# Optimizing a Trainium2 kernel written in Bass

```python
import numpy as np
import jax
import jax.numpy as jnp

def _softmax(x, axis=-1):
    return jax.nn.softmax(x, axis=axis)

def _gelu(x):
    return jax.nn.gelu(x, approximate=True)

def _silu(x):
    return jax.nn.silu(x)

def _sigmoid(x):
    return jax.nn.sigmoid(x)

def _layernorm(x, axis=-1, eps=1e-05):
    m = jnp.mean(x, axis=axis, keepdims=True)
    v = jnp.var(x, axis=axis, keepdims=True)
    return (x - m) / jnp.sqrt(v + eps)

def _scatter_add(tgt, idx, src, axis=0):
    return tgt.at[idx].add(src)

def _segment_sum(src, seg, n):
    return jax.ops.segment_sum(src, seg, n)
kernel_name = 'mk_cond_seq_d2_seqx_r8_fcdfd9'

def setup_inputs(seed: int=0):
    np.random.seed(seed)
    _w = jnp.asarray

    def _rec_inputs():
        import jax
        import jax.numpy as jnp
        _rk = jax.random.key(seed)
        x = 0.4999 + 0.2886 * jax.random.normal(jax.random.fold_in(_rk, 1), (8, 128, 128), jnp.float32)
        _lenS = 128 - jax.random.randint(jax.random.fold_in(_rk, 7), (8,), 0, max(1, 128 // 4) + 1, jnp.int32)
        _lenS2 = 128 - jax.random.randint(jax.random.fold_in(_rk, 8), (8,), 0, max(1, 128 // 4) + 1, jnp.int32)
        condB_dt = jax.random.uniform(jax.random.fold_in(_rk, 11), (8,), jnp.float32, 0.0, 0.981965)
        itok_B_6_14 = jax.random.randint(jax.random.fold_in(_rk, 12), (8,), 6, 15, jnp.int32)
        return (x, condB_dt, itok_B_6_14)
    x, condB_dt, itok_B_6_14 = _rec_inputs()

    def _L0_cond_setup():
        import jax, jax.numpy as jnp
        import numpy as np
        B, NX, NY = (16, 128, 128)

        def _grad(f, axis):
            fm = jnp.moveaxis(f, axis, -1)
            g = (jnp.roll(fm, -1, -1) - jnp.roll(fm, 1, -1)) * 0.5
            g0 = (-3.0 * fm[..., 0] + 4.0 * fm[..., 1] - fm[..., 2]) * 0.5
            gN = (3.0 * fm[..., -1] - 4.0 * fm[..., -2] + fm[..., -3]) * 0.5
            g = g.at[..., 0].set(g0).at[..., -1].set(gN)
            return jnp.moveaxis(g, -1, axis)

        def _grad2(f, axis):
            fm = jnp.moveaxis(f, axis, -1)
            g = jnp.roll(fm, -1, -1) - 2.0 * fm + jnp.roll(fm, 1, -1)
            g0 = 2.0 * fm[..., 0] - 5.0 * fm[..., 1] + 4.0 * fm[..., 2] - fm[..., 3]
            gN = 2.0 * fm[..., -1] - 5.0 * fm[..., -2] + 4.0 * fm[..., -3] - fm[..., -4]
            g = g.at[..., 0].set(g0).at[..., -1].set(gN)
            return jnp.moveaxis(g, -1, axis)
        key = jax.random.key(seed)
        k1, k2, k3, k4 = jax.random.split(key, 4)
        f = jax.random.uniform(k1, (B, NX, NY), dtype=jnp.float32)
        A_grid = jax.random.normal(k2, (2, NX, NY), dtype=jnp.float32)
        B_grid = jax.random.uniform(k3, (3, NX, NY), dtype=jnp.float32)
        dt = jax.random.uniform(k4, (B,), dtype=jnp.float32)
        return {'f': f, 'A_grid': A_grid, 'B_grid': B_grid, 'dt': dt}
    _L0_cond_all = _L0_cond_setup()
    _L0_cond_in = {k: v for k, v in _L0_cond_all.items() if k in ('A_grid', 'B_grid')}
    del _L0_cond_all

    def _L1_cond_setup():
        import jax, jax.numpy as jnp
        import numpy as np
        D = 128
        E = 8
        FF = 512
        TOPK = 2
        S = 32
        SE = 64
        SH = 128
        B, T = (2, 256)

        def _forward(x, subject_ids, ln_g, ln_b, subj_emb, hyp_w1, hyp_b1, hyp_w2, hyp_b2, sty_w1, sty_b1, sty_w2, sty_b2, router_w, exp_w1, exp_b1, exp_w2, exp_b2):
            mu = x.mean(-1, keepdims=True)
            var = x.var(-1, keepdims=True)
            h = (x - mu) * jax.lax.rsqrt(var + 1e-05) * ln_g + ln_b
            m_t = h.mean(1, keepdims=True)
            v_t = h.var(1, keepdims=True)
            h_norm = (h - m_t) * jax.lax.rsqrt(v_t + 1e-08)
            se = subj_emb[subject_ids]
            hyp = jax.nn.relu(se @ hyp_w1 + hyp_b1) @ hyp_w2 + hyp_b2
            sty = jax.nn.relu(hyp @ sty_w1 + sty_b1) @ sty_w2 + sty_b2
            gamma, beta = jnp.split(sty, 2, axis=-1)
            gamma = jax.nn.softplus(gamma) + 1e-08
            h = h_norm * gamma[:, None, :] + beta[:, None, :]
            h_flat = h.reshape(-1, D)
            probs = jax.nn.softmax(h_flat @ router_w, axis=-1)
            gates, idx = jax.lax.top_k(probs, TOPK)
            gates = gates / gates.sum(-1, keepdims=True)
            N = h_flat.shape[0]
            combine = jnp.zeros((N, E), h_flat.dtype).at[jnp.arange(N)[:, None], idx].add(gates)
            hid = jax.nn.relu(jnp.einsum('nd,edf->nef', h_flat, exp_w1) + exp_b1)
            eout = jnp.einsum('nef,efd->ned', hid, exp_w2) + exp_b2
            y = jnp.einsum('ned,ne->nd', eout, combine)
            return x + y.reshape(x.shape)
        key = jax.random.key(seed)
        ks = jax.random.split(key, 16)
        n = lambda k, sh, s=0.02: jax.random.normal(k, sh, dtype=jnp.float32) * s
        return {'x': jax.random.normal(ks[0], (B, T, D), dtype=jnp.float32), 'subject_ids': jax.random.randint(ks[1], (B,), 0, S), 'ln_g': jnp.ones((D,), jnp.float32), 'ln_b': jnp.zeros((D,), jnp.float32), 'subj_emb': n(ks[2], (S, SE)), 'hyp_w1': n(ks[3], (SE, SH), 1.0 / np.sqrt(SE)), 'hyp_b1': jnp.zeros((SH,), jnp.float32), 'hyp_w2': n(ks[4], (SH, SH), 1.0 / np.sqrt(SH)), 'hyp_b2': jnp.zeros((SH,), jnp.float32), 'sty_w1': n(ks[5], (SH, SH // 2), 1.0 / np.sqrt(SH)), 'sty_b1': jnp.zeros((SH // 2,), jnp.float32), 'sty_w2': n(ks[6], (SH // 2, 2 * D), 1.0 / np.sqrt(SH // 2)), 'sty_b2': jnp.zeros((2 * D,), jnp.float32), 'router_w': n(ks[7], (D, E), 1.0 / np.sqrt(D)), 'exp_w1': n(ks[8], (E, D, FF), 1.0 / np.sqrt(D)), 'exp_b1': jnp.zeros((E, FF), jnp.float32), 'exp_w2': n(ks[9], (E, FF, D), 1.0 / np.sqrt(FF)), 'exp_b2': jnp.zeros((E, D), jnp.float32)}
    _L1_cond_all = _L1_cond_setup()
    _L1_cond_in = {k: v for k, v in _L1_cond_all.items() if k in ('ln_g', 'ln_b', 'subj_emb', 'hyp_w1', 'hyp_b1', 'hyp_w2', 'hyp_b2', 'sty_w1', 'sty_b1', 'sty_w2', 'sty_b2', 'router_w', 'exp_w1', 'exp_b1', 'exp_w2', 'exp_b2')}
    del _L1_cond_all
    return {'x': x, 'condB_dt': condB_dt, 'itok_B_6_14': itok_B_6_14, 'L0_cond_A_grid': _L0_cond_in['A_grid'], 'L0_cond_B_grid': _L0_cond_in['B_grid'], 'L1_cond_ln_g': _L1_cond_in['ln_g'], 'L1_cond_ln_b': _L1_cond_in['ln_b'], 'L1_cond_subj_emb': _L1_cond_in['subj_emb'], 'L1_cond_hyp_w1': _L1_cond_in['hyp_w1'], 'L1_cond_hyp_b1': _L1_cond_in['hyp_b1'], 'L1_cond_hyp_w2': _L1_cond_in['hyp_w2'], 'L1_cond_hyp_b2': _L1_cond_in['hyp_b2'], 'L1_cond_sty_w1': _L1_cond_in['sty_w1'], 'L1_cond_sty_b1': _L1_cond_in['sty_b1'], 'L1_cond_sty_w2': _L1_cond_in['sty_w2'], 'L1_cond_sty_b2': _L1_cond_in['sty_b2'], 'L1_cond_router_w': _L1_cond_in['router_w'], 'L1_cond_exp_w1': _L1_cond_in['exp_w1'], 'L1_cond_exp_b1': _L1_cond_in['exp_b1'], 'L1_cond_exp_w2': _L1_cond_in['exp_w2'], 'L1_cond_exp_b2': _L1_cond_in['exp_b2']}

def reference(x, condB_dt, itok_B_6_14, L0_cond_A_grid, L0_cond_B_grid, L1_cond_ln_g, L1_cond_ln_b, L1_cond_subj_emb, L1_cond_hyp_w1, L1_cond_hyp_b1, L1_cond_hyp_w2, L1_cond_hyp_b2, L1_cond_sty_w1, L1_cond_sty_b1, L1_cond_sty_w2, L1_cond_sty_b2, L1_cond_router_w, L1_cond_exp_w1, L1_cond_exp_b1, L1_cond_exp_w2, L1_cond_exp_b2):
    import jax
    import jax.numpy as jnp

    def _L0_cond_ref(f, A_grid, B_grid, dt):
        import jax, jax.numpy as jnp
        import numpy as np
        B, NX, NY = (16, 128, 128)

        def _grad(f, axis):
            fm = jnp.moveaxis(f, axis, -1)
            g = (jnp.roll(fm, -1, -1) - jnp.roll(fm, 1, -1)) * 0.5
            g0 = (-3.0 * fm[..., 0] + 4.0 * fm[..., 1] - fm[..., 2]) * 0.5
            gN = (3.0 * fm[..., -1] - 4.0 * fm[..., -2] + fm[..., -3]) * 0.5
            g = g.at[..., 0].set(g0).at[..., -1].set(gN)
            return jnp.moveaxis(g, -1, axis)

        def _grad2(f, axis):
            fm = jnp.moveaxis(f, axis, -1)
            g = jnp.roll(fm, -1, -1) - 2.0 * fm + jnp.roll(fm, 1, -1)
            g0 = 2.0 * fm[..., 0] - 5.0 * fm[..., 1] + 4.0 * fm[..., 2] - fm[..., 3]
            gN = 2.0 * fm[..., -1] - 5.0 * fm[..., -2] + 4.0 * fm[..., -3] - fm[..., -4]
            g = g.at[..., 0].set(g0).at[..., -1].set(gN)
            return jnp.moveaxis(g, -1, axis)
        Af = A_grid[None] * f[:, None]
        Bf = B_grid[None] * f[:, None]
        gradv_Af = _grad(Af[:, 0], 1) + _grad(Af[:, 1], 2)
        gradvv_Bf = _grad2(Bf[:, 0], 1) + _grad2(Bf[:, 1], 2) + _grad(_grad(Bf[:, 2], 2), 1) + _grad(_grad(Bf[:, 2], 1), 2)
        df = -gradv_Af + gradvv_Bf * 0.5
        f_new = f + df * dt[:, None, None]
        return jnp.maximum(f_new, 0.0)

    def _L1_cond_ref(x, subject_ids, ln_g, ln_b, subj_emb, hyp_w1, hyp_b1, hyp_w2, hyp_b2, sty_w1, sty_b1, sty_w2, sty_b2, router_w, exp_w1, exp_b1, exp_w2, exp_b2):
        import jax, jax.numpy as jnp
        import numpy as np
        D = 128
        E = 8
        FF = 512
        TOPK = 2
        S = 32
        SE = 64
        SH = 128
        B, T = (2, 256)

        def _forward(x, subject_ids, ln_g, ln_b, subj_emb, hyp_w1, hyp_b1, hyp_w2, hyp_b2, sty_w1, sty_b1, sty_w2, sty_b2, router_w, exp_w1, exp_b1, exp_w2, exp_b2):
            mu = x.mean(-1, keepdims=True)
            var = x.var(-1, keepdims=True)
            h = (x - mu) * jax.lax.rsqrt(var + 1e-05) * ln_g + ln_b
            m_t = h.mean(1, keepdims=True)
            v_t = h.var(1, keepdims=True)
            h_norm = (h - m_t) * jax.lax.rsqrt(v_t + 1e-08)
            se = subj_emb[subject_ids]
            hyp = jax.nn.relu(se @ hyp_w1 + hyp_b1) @ hyp_w2 + hyp_b2
            sty = jax.nn.relu(hyp @ sty_w1 + sty_b1) @ sty_w2 + sty_b2
            gamma, beta = jnp.split(sty, 2, axis=-1)
            gamma = jax.nn.softplus(gamma) + 1e-08
            h = h_norm * gamma[:, None, :] + beta[:, None, :]
            h_flat = h.reshape(-1, D)
            probs = jax.nn.softmax(h_flat @ router_w, axis=-1)
            gates, idx = jax.lax.top_k(probs, TOPK)
            gates = gates / gates.sum(-1, keepdims=True)
            N = h_flat.shape[0]
            combine = jnp.zeros((N, E), h_flat.dtype).at[jnp.arange(N)[:, None], idx].add(gates)
            hid = jax.nn.relu(jnp.einsum('nd,edf->nef', h_flat, exp_w1) + exp_b1)
            eout = jnp.einsum('nef,efd->ned', hid, exp_w2) + exp_b2
            y = jnp.einsum('ned,ne->nd', eout, combine)
            return x + y.reshape(x.shape)
        return _forward(x, subject_ids, ln_g, ln_b, subj_emb, hyp_w1, hyp_b1, hyp_w2, hyp_b2, sty_w1, sty_b1, sty_w2, sty_b2, router_w, exp_w1, exp_b1, exp_w2, exp_b2)
    x = _L0_cond_ref(x, L0_cond_A_grid, L0_cond_B_grid, condB_dt)
    x = _L1_cond_ref(x, itok_B_6_14, L1_cond_ln_g, L1_cond_ln_b, L1_cond_subj_emb, L1_cond_hyp_w1, L1_cond_hyp_b1, L1_cond_hyp_w2, L1_cond_hyp_b2, L1_cond_sty_w1, L1_cond_sty_b1, L1_cond_sty_w2, L1_cond_sty_b2, L1_cond_router_w, L1_cond_exp_w1, L1_cond_exp_b1, L1_cond_exp_w2, L1_cond_exp_b2)
    return x

_drawn_inputs = setup_inputs


def setup_inputs(seed=0):
    import zlib

    import numpy as np

    out = dict(_drawn_inputs(seed))
    spreads = {'L1_cond_ln_g': (1.0, 0.2),
     'L1_cond_ln_b': (0.0, 0.1),
     'L1_cond_hyp_b1': (0.0, 0.1),
     'L1_cond_hyp_b2': (0.0, 0.1),
     'L1_cond_sty_b1': (0.0, 0.1),
     'L1_cond_sty_b2': (0.0, 0.1),
     'L1_cond_exp_b1': (0.0, 0.1),
     'L1_cond_exp_b2': (0.0, 0.1)}
    factors = {}
    for name, (base, spread) in spreads.items():
        noise = np.random.default_rng([zlib.crc32(name.encode()), seed]).standard_normal(out[name].shape)
        drawn = base * np.exp(spread * noise) if base else spread * noise
        out[name] = jnp.asarray(drawn.astype(out[name].dtype))
    for name, factor in factors.items():
        out[name] = (out[name] * factor).astype(out[name].dtype)
    return out
```

```python
from contextlib import ExitStack

import numpy as np

import concourse.bass as bass
from concourse import mybir

F32 = mybir.dt.float32
F32R = mybir.dt.float32r
I32 = mybir.dt.int32
ALU = mybir.AluOpType
ACT = mybir.ActivationFunctionType
AX = mybir.AxisListType

P = 128
B = 8
BH = B // 2
HALVES = 2
HT = BH * P
T = B * P
E = 8
FF = 512
C = FF // P
NS = 32
SE = 64
SH = 128
G16 = 2 * E
LAG = 3
SLOTS = 2

IDENT, DIFF, HALF_DIFF2 = range(3)
NMAT = 3
LN_G, LN_B, HYP_B1, HYP_B2, STY_BG, STY_BB = range(6)
RW_AT = 6
HW2_AT = RW_AT + E
SW1_AT = HW2_AT + SH
B1_AT = SW1_AT + SE
N128 = B1_AT + E * C
STY_B1 = 0
HW1_AT = 1
SW2_AT = HW1_AT + SH
EMB_AT = SW2_AT + 2 * P
N64 = EMB_AT + SE


def constants():
    d = np.zeros((P, P), np.float32)
    d2 = np.zeros((P, P), np.float32)
    for m in range(1, P - 1):
        d[m, m + 1], d[m, m - 1] = 0.5, -0.5
        d2[m, m + 1], d2[m, m], d2[m, m - 1] = 1.0, -2.0, 1.0
    d[0, 0:3] = -1.5, 2.0, -0.5
    d[P - 1, P - 3:P] = 0.5, -2.0, 1.5
    d2[0, 0:4] = 2.0, -5.0, 4.0, -1.0
    d2[P - 1, P - 4:P] = -1.0, 4.0, -5.0, 2.0
    mats = np.stack([np.eye(P, dtype=np.float32), d.T, 0.5 * d2.T], axis=1)
    sel = np.zeros((G16, E, P), np.float32)
    for e in range(E):
        sel[e, e] = sel[E + e, e] = 1.0
    return np.ascontiguousarray(mats), sel


def build(nc, const, selectors, x, xT, grids, gridsT, dt, ids, p128, p64, exp_w, exp_b2, out):
    with ExitStack() as ctx:
        def sb(name, shape, dtype=F32):
            return ctx.enter_context(nc.sbuf_tensor(name, shape, dtype))

        def sem(name):
            return ctx.enter_context(nc.semaphore(name))

        mats = sb("mats", [P, NMAT, P])
        sel_all = sb("sel_all", [G16, E, P])
        f = sb("f", [P, B, P])
        ft = sb("ft", [P, B, P])
        gn = sb("gn", [P, 3, P])
        gt = sb("gt", [P, 2, P])
        dtb = sb("dtb", [P, B])
        idi = sb("idi", [NS, B], I32)
        pv = sb("pv", [P, N128])
        pw = sb("pw", [SE, N64])
        b2_rows = sb("b2_rows", [G16, P])
        we = sb("we", [P, E, 2, C, P])
        neg_a0 = sb("neg_a0", [P, P])
        s_b2 = sb("s_b2", [P, B, P])
        u_a0 = sb("u_a0", [P, B, P])
        u_b0 = sb("u_b0", [P, B, P])
        u_a1 = sb("u_a1", [P, B, P])
        u_b1 = sb("u_b1", [P, B, P])
        wT = sb("wT", [P, B, P])
        xp = sb("xp", [P, B, P])
        xs = sb("xs", [P, B, P])
        st1 = sb("st1", [P, B, 6])
        mv1 = sb("mv1", [P, B, 2])
        sd1 = sb("sd1", [P, B])
        rs1 = sb("rs1", [P, B])
        xn = sb("xn", [P, B, P])
        st2 = sb("st2", [P, B, 6])
        mv2 = sb("mv2", [P, B, 2])
        gsq = sb("gsq", [P, 1])
        vh = sb("vh", [P, B])
        mh = sb("mh", [P, B])
        dmean = sb("dmean", [P, B])
        sd2 = sb("sd2", [P, B])
        rs2 = sb("rs2", [P, B])
        tg = sb("tg", [P, B])
        scale = sb("scale", [P, B])
        shift0 = sb("shift0", [P, B])
        shift = sb("shift", [P, B])
        h = sb("h", [P, T])
        h_hi = sb("h_hi", [P, T], F32R)
        h_lo = sb("h_lo", [P, T], F32R)
        idf = sb("idf", [NS, B])
        idn = sb("idn", [NS, B])
        idw = sb("idw", [NS, B])
        idc = sb("idc", [NS, B])
        row_no = sb("row_no", [NS, 1])
        onehot = sb("onehot", [NS, B])
        se = sb("se", [SE, B])
        hyp1 = sb("hyp1", [SH, B])
        hyp2 = sb("hyp2", [SH, B])
        sty1 = sb("sty1", [SE, B])
        graw = sb("graw", [P, B])
        beta = sb("beta", [P, B])
        gabs = sb("gabs", [P, B])
        gexp = sb("gexp", [P, B])
        glog = sb("glog", [P, B])
        gpos = sb("gpos", [P, B])
        gsum = sb("gsum", [P, B])
        gamma = sb("gamma", [P, B])
        b1s = sb("b1s", [P, SLOTS, C])
        gneg = sb("gneg", [P, B])
        eps_ln = sb("eps_ln", [P, 1])
        eps_t = sb("eps_t", [P, 1])
        one = sb("one", [P, 1])
        rank = sb("rank", [P, E])
        lmax = sb("lmax", [P, B])
        ld = sb("ld", [P, B, E])
        pe_ = sb("pe_", [P, B, E])
        z = sb("z", [P, B])
        rz = sb("rz", [P, B])
        pr = sb("pr", [P, B, E])
        m1 = sb("m1", [P, B])
        eq1 = sb("eq1", [P, B, E])
        rk1 = sb("rk1", [P, B, E])
        rm1 = sb("rm1", [P, B])
        o1 = sb("o1", [P, B, E])
        rest = sb("rest", [P, B, E])
        m2 = sb("m2", [P, B])
        eq2 = sb("eq2", [P, B, E])
        rk2 = sb("rk2", [P, B, E])
        rm2 = sb("rm2", [P, B])
        o2 = sb("o2", [P, B, E])
        o12 = sb("o12", [P, B, E])
        pk = sb("pk", [P, B, E])
        ps = sb("ps", [P, B])
        rps = sb("rps", [P, B])
        gate = sb("gate", [P, B, E])
        gate_parts = sb("gate_parts", [P, B, G16], F32R)
        gateT = sb("gateT", [G16, T], F32R)
        ws = sb("ws", [P, SLOTS, 2, 2, C, P], F32R)
        sel = sb("sel", [G16, SLOTS, P], F32R)
        hid = sb("hid", [P, C, T])
        hid_hi = sb("hid_hi", [P, C, T], F32R)
        hid_lo = sb("hid_lo", [P, C, T], F32R)
        gate_all = sb("gate_all", [P, T])
        yg = sb("yg", [P, T])
        acc = sb("acc", [P, T])

        zt = [ctx.enter_context(nc.psum_tensor(f"zt{n}", [P, T], F32)) for n in range(2)]
        yt = ctx.enter_context(nc.psum_tensor("yt", [P, T], F32))
        aux = ctx.enter_context(nc.psum_tensor("aux", [P, T], F32))

        def bank(t, n):
            return t[:, n * HT:(n + 1) * HT]

        xsT = [bank(zt[0], n) for n in range(HALVES)]
        rT = [bank(zt[1], n) for n in range(HALVES)]
        df = [bank(yt, n) for n in range(HALVES)]
        xnT = [bank(aux, n) for n in range(HALVES)]
        small = bank(aux, 0)
        ident = mats[:, IDENT, :]

        mats_in = sem("mats_in")
        f_in = [sem(f"f_in{n}") for n in range(HALVES)]
        ft_in = [sem(f"ft_in{n}") for n in range(HALVES)]
        gn_in = sem("gn_in")
        gt_in = sem("gt_in")
        dt_in = sem("dt_in")
        p128_in = sem("p128_in")
        p64_in = sem("p64_in")
        ids_in = sem("ids_in")
        rows_in = sem("rows_in")
        ROWS_DMAS = 3
        w_in = [sem(f"w_in{n}") for n in range(3)]
        out_done = sem("out_done")
        pool_chain = sem("pool_chain")
        onehot_ready = sem("onehot_ready")
        const_ready = sem("const_ready")
        gamma_ready = sem("gamma_ready")
        gabs_ready = sem("gabs_ready")
        net_ps = sem("net_ps")
        net_sb = sem("net_sb")
        soft_steps = sem("soft_steps")
        prod_ready = sem("prod_ready")
        rT_ready = sem("rT_ready")
        df_ready = sem("df_ready")
        xp_ready = sem("xp_ready")
        xs_ready = sem("xs_ready")
        dve = sem("dve")
        var1_ready = sem("var1_ready")
        sd1_ready = sem("sd1_ready")
        xn_ready = sem("xn_ready")
        xnT_ready = sem("xnT_ready")
        var2_ready = sem("var2_ready")
        sd2_ready = sem("sd2_ready")
        h_ready = sem("h_ready")
        h_hi_ready = sem("h_hi_ready")
        h_lo_ready = sem("h_lo_ready")
        logits_ready = sem("logits_ready")
        ld_ready = sem("ld_ready")
        exp_ready = sem("exp_ready")
        parts_ready = sem("parts_ready")
        gateT_ps = sem("gateT_ps")
        gateT_ready = sem("gateT_ready")
        bias_ps = sem("bias_ps")
        acc_ready = sem("acc_ready")
        w_hi_ready = sem("w_hi_ready")
        w_ready = sem("w_ready")
        b1_ready = sem("b1_ready")
        xsT_ready = sem("xsT_ready")
        sel_ready = sem("sel_ready")
        z_ready = sem("z_ready")
        hi_ready = sem("hi_ready")
        hid_ready = sem("hid_ready")
        lo_ready = sem("lo_ready")
        l2_done = sem("l2_done")
        y_half = sem("y_half")
        yg_half = sem("yg_half")
        acc_half = sem("acc_half")
        gate_ps = sem("gate_ps")
        gate_ready = sem("gate_ready")

        block = ctx.enter_context(nc.Block())

        @block.sync
        def _(sp):
            def load(tile, source, done):
                sp.dma_start(tile, source).then_inc(done, 16)

            load(gn[:], grids, gn_in)
            load(f[:, 0:BH, :], x[:, 0:BH, :], f_in[0])
            load(mats[:], const, mats_in)
            load(gt[:], gridsT, gt_in)
            load(ft[:, 0:BH, :], xT[:, 0:BH, :], ft_in[0])
            load(f[:, BH:B, :], x[:, BH:B, :], f_in[1])
            load(ft[:, BH:B, :], xT[:, BH:B, :], ft_in[1])
            for e in range(E):
                load(we[:, e], exp_w[e], w_in[min(e, 2)])
            for n in range(HALVES):
                tok = slice(n * HT, (n + 1) * HT)
                sp.wait_ge(acc_half, HALVES * (E - 1) + n + 1 + HALVES)
                sp.dma_start(out[:, tok], acc[:, tok]).then_inc(out_done, 16)
            sp.wait_ge(out_done, 16 * HALVES)

        @block.gpsimd
        def _(pool):
            steps = [0]

            def step(ins):
                steps[0] += 1
                ins.then_inc(pool_chain, 1)
                pool.wait_ge(pool_chain, steps[0])

            pool.memset(eps_ln[:], 1e-5).then_inc(const_ready, 1)
            pool.memset(eps_t[:], 1e-8).then_inc(const_ready, 1)
            pool.memset(one[:], 1.0).then_inc(const_ready, 1)
            pool.iota(rank[:], pattern=[[-1, E]], base=E, channel_multiplier=0,
                      allow_small_or_imprecise_dtypes=True).then_inc(const_ready, 1)
            step(pool.iota(row_no[:], pattern=[[0, 1]], base=0, channel_multiplier=1,
                           allow_small_or_imprecise_dtypes=True))
            pool.wait_ge(ids_in, 16)
            step(pool.tensor_copy(idf[:], idi[:]))
            step(pool.tensor_scalar(idn[:], idf[:], 0.0, float(NS), ALU.is_lt, ALU.mult))
            step(pool.tensor_tensor(idw[:], idf[:], idn[:], ALU.add))
            step(pool.tensor_scalar(idc[:], idw[:], float(NS - 1), 0.0, ALU.min, ALU.max))
            pool.tensor_scalar(onehot[:], idc[:], row_no[:, 0:1], None, ALU.is_equal).then_inc(onehot_ready, 1)
            pool.wait_ge(soft_steps, 2)
            pool.tensor_tensor(gabs[:], gpos[:], gneg[:], ALU.add).then_inc(gabs_ready, 1)
            for e in range(SLOTS):
                pool.wait_ge(w_in[e], 16)
                for layer in range(2):
                    step(pool.tensor_scalar(ws[:, e, 0, layer], we[:, e, layer], 1.0, 0.0, ALU.mult, ALU.add))
                    last = pool.tensor_tensor(ws[:, e, 1, layer], we[:, e, layer], ws[:, e, 0, layer].bitcast(F32),
                                              ALU.subtract)
                    if layer == 0:
                        steps[0] += 1
                        last.then_inc(pool_chain, 1)
                last.then_inc(w_ready, 1)
                pool.wait_ge(pool_chain, steps[0])
                if e == 0:
                    pool.wait_ge(soft_steps, 4)
                    step(pool.tensor_tensor(gsum[:], gpos[:], glog[:], ALU.add))
                    pool.tensor_scalar(gamma[:], gsum[:], 1e-8, None, ALU.add).then_inc(gamma_ready, 1)

        @block.scalar
        def _(act):
            act.dma_start(idi[:], ids.partition_broadcast(NS)).then_inc(ids_in, 16)
            act.dma_start(pw[:], p64).then_inc(p64_in, 16)
            act.dma_start(pv[:], p128).then_inc(p128_in, 16)
            act.dma_start(dtb[:], dt.partition_broadcast(P)).then_inc(dt_in, 16)
            for n in range(2):
                act.dma_start(b2_rows[n * E:(n + 1) * E, :], exp_b2).then_inc(rows_in, 16)
            act.dma_start(sel_all[:], selectors).then_inc(rows_in, 16)
            act.wait_ge(const_ready, 4)
            act.wait_ge(p128_in, 16)
            act.wait_ge(p64_in, 16)
            act.wait_ge(net_ps, 1)
            act.activation(se[:], small[0:SE, 0:B], ACT.Copy).then_inc(net_sb, 1)
            act.wait_ge(net_ps, 2)
            act.activation(hyp1[:], small[:, 0:B], ACT.Relu, bias=pv[:, HYP_B1:HYP_B1 + 1]).then_inc(net_sb, 1)
            act.wait_ge(net_ps, 3)
            act.activation(hyp2[:], small[:, 0:B], ACT.Identity, bias=pv[:, HYP_B2:HYP_B2 + 1]).then_inc(net_sb, 1)
            act.wait_ge(net_ps, 4)
            act.activation(sty1[:], small[0:SE, 0:B], ACT.Relu, bias=pw[:, STY_B1:STY_B1 + 1]).then_inc(net_sb, 1)
            act.wait_ge(net_ps, 5)
            act.activation(graw[:], small[:, 0:B], ACT.Identity, bias=pv[:, STY_BG:STY_BG + 1]).then_inc(net_sb, 1)
            act.activation(beta[:], small[:, B:2 * B], ACT.Identity, bias=pv[:, STY_BB:STY_BB + 1]).then_inc(net_sb, 1)
            act.wait_ge(net_sb, 6)
            act.activation(gpos[:], graw[:], ACT.Relu).then_inc(soft_steps, 1)
            act.activation(gneg[:], graw[:], ACT.Relu, scale=-1.0).then_inc(soft_steps, 1)
            act.wait_ge(gabs_ready, 1)
            act.activation(gexp[:], gabs[:], ACT.Exp, scale=-1.0).then_inc(soft_steps, 1)
            act.wait_ge(soft_steps, 3)
            act.activation(glog[:], gexp[:], ACT.Ln, bias=one[:, 0:1]).then_inc(soft_steps, 1)

            def relu_step(n):
                act.wait_ge(xp_ready, BH * (n + 1))
                act.activation(xs[:, n * BH:(n + 1) * BH, :], xp[:, n * BH:(n + 1) * BH, :], ACT.Relu).then_inc(xs_ready, 1)

            def sd_features(n):
                act.wait_ge(var1_ready, BH * (n + 1))
                act.activation(sd1[:, n * BH:(n + 1) * BH], mv1[:, n * BH:(n + 1) * BH, 1], ACT.Sqrt,
                               bias=eps_ln[:, 0:1]).then_inc(sd1_ready, 1)

            def sd_tokens(n):
                act.wait_ge(var2_ready, n + 1)
                act.activation(sd2[:, n * BH:(n + 1) * BH], vh[:, n * BH:(n + 1) * BH], ACT.Sqrt,
                               bias=eps_t[:, 0:1]).then_inc(sd2_ready, 1)

            def transposed_step(n):
                act.wait_ge(xsT_ready, n + 1)
                act.activation(acc[:, n * HT:(n + 1) * HT], xsT[n], ACT.Copy).then_inc(acc_ready, 1)

            relu_step(0)
            sd_features(0)
            transposed_step(0)
            sd_tokens(0)
            relu_step(1)
            sd_features(1)
            transposed_step(1)
            sd_tokens(1)
            act.wait_ge(ld_ready, 1)
            act.activation(pe_[:], ld[:], ACT.Exp).then_inc(exp_ready, 1)

            def hidden(e, c, slot, start):
                g = C * e + c
                act.wait_ge(z_ready, g + 1)
                if not start:
                    if c < C - 1:
                        act.wait_ge(l2_done, (C - 1) * (e - 1) + c + 1)
                    else:
                        act.wait_ge(y_half, HALVES * e)
                bias = b1s[:, slot, c:c + 1]
                if c == 0:
                    act.wait_ge(b1_ready, e + 1)
                act.activation(hid_hi[:, c, :], zt[c % 2][:], ACT.Relu, bias=bias).then_inc(hi_ready, 1)
                if not start:
                    act.wait_ge(lo_ready, g - C + 1)
                act.activation(hid[:, c, :], zt[c % 2][:], ACT.Relu, bias=bias).then_inc(hid_ready, 1)

            def gates_out(e, start):
                act.wait_ge(gate_ps, e + 1)
                if not start:
                    act.wait_ge(yg_half, HALVES * e)
                act.activation(gate_all[:], aux[:], ACT.Copy).then_inc(gate_ready, 1)

            def pair(i, first=False):
                for k in range(2):
                    e = 2 * i + k
                    for c in range(C):
                        hidden(e, c, k, first and k == 0)
                        if first and k == 0 and c == 0:
                            act.wait_ge(gateT_ps, 1)
                            act.activation(gateT[:], aux[0:G16, :], ACT.Copy).then_inc(gateT_ready, 1)
                        if c == C - 1:
                            gates_out(e, first and k == 0)

            pair(0, first=True)
            with act.Fori(1, E // 2) as i:
                pair(i)

        @block.tensor
        def _(pe):
            def step_cross(n):
                if n == 0:
                    pe.wait_ge(mats_in, 16)
                pe.wait_ge(prod_ready, 6 * n + 1)
                for b in range(BH):
                    last = pe.matmul(rT[n][:, b * P:(b + 1) * P], s_b2[:, n * BH + b, :], mats[:, DIFF, :],
                                     start=True, stop=True)
                last.then_inc(rT_ready, 1)

            def step_rows(n):
                hb = slice(n * BH, (n + 1) * BH)
                pe.wait_ge(prod_ready, 6 * n + 2)
                pe.matmul(df[n], mats[:, DIFF, :], u_a0[:, hb, :].rearrange("p b j -> p (b j)"),
                          start=True, stop=False, skip_group_check=True)
                pe.wait_ge(prod_ready, 6 * n + 3)
                pe.matmul(df[n], mats[:, HALF_DIFF2, :], u_b0[:, hb, :].rearrange("p b j -> p (b j)"),
                          start=False, stop=False, skip_group_check=True)

            def step_columns(n):
                pe.wait_ge(prod_ready, 6 * n + 4)
                for b in range(BH):
                    pe.matmul(df[n][:, b * P:(b + 1) * P], u_b1[:, n * BH + b, :], mats[:, HALF_DIFF2, :],
                              start=False, stop=False, skip_group_check=True)
                pe.wait_ge(prod_ready, 6 * n + 6)
                for b in range(BH):
                    last = pe.matmul(df[n][:, b * P:(b + 1) * P], wT[:, n * BH + b, :], mats[:, DIFF, :],
                                     start=False, stop=(b == BH - 1), skip_group_check=True)
                last.then_inc(df_ready, 1)

            def net_layer(n, weights, acts, rows):
                pe.matmul(small[0:rows, 0:B], weights, acts, start=True, stop=True).then_inc(net_ps, 1)

            pe.wait_ge(onehot_ready, 1)
            pe.wait_ge(p64_in, 16)
            net_layer(0, pw[0:NS, EMB_AT:EMB_AT + SE], onehot[:], SE)
            pe.wait_ge(net_sb, 1)
            net_layer(1, pw[:, HW1_AT:HW1_AT + SH], se[:], SH)
            step_cross(0)
            pe.wait_ge(p128_in, 16)
            pe.wait_ge(net_sb, 2)
            net_layer(2, pv[:, HW2_AT:HW2_AT + SH], hyp1[:], SH)
            step_rows(0)
            pe.wait_ge(net_sb, 3)
            net_layer(3, pv[:, SW1_AT:SW1_AT + SE], hyp2[:], SE)
            step_columns(0)
            pe.wait_ge(net_sb, 4)
            pe.matmul(small[:, 0:B], pw[:, SW2_AT:SW2_AT + P], sty1[:], start=True, stop=True)
            pe.matmul(small[:, B:2 * B], pw[:, SW2_AT + P:SW2_AT + 2 * P], sty1[:], start=True,
                      stop=True).then_inc(net_ps, 1)
            step_cross(1)
            step_rows(1)

            def step_transposed(n):
                pe.wait_ge(xs_ready, n + 1)
                for b in range(BH):
                    last = pe.transpose(xsT[n][:, b * P:(b + 1) * P], xs[:, n * BH + b, :], ident)
                last.then_inc(xsT_ready, 1)

            def norm_transposed(n):
                pe.wait_ge(xn_ready, BH * (n + 1))
                if n == 0:
                    pe.wait_ge(net_sb, 6)
                for b in range(BH):
                    last = pe.transpose(xnT[n][:, b * P:(b + 1) * P], xn[:, n * BH + b, :], ident)
                last.then_inc(xnT_ready, 1)

            step_transposed(0)
            norm_transposed(0)
            step_columns(1)
            norm_transposed(1)
            step_transposed(1)
            pe.wait_ge(h_ready, B)
            for b in range(B):
                last = pe.matmul(small[:, b * E:(b + 1) * E], h[:, b * P:(b + 1) * P], pv[:, RW_AT:RW_AT + E], start=True, stop=True)
            last.then_inc(logits_ready, 1)

            def layer1(e, c, slot):
                g = C * e + c
                if c == 0:
                    pe.wait_ge(w_ready, e + 1)
                out_ps = zt[c % 2]
                w_hi, w_lo = ws[:, slot, 0, 0, c, :], ws[:, slot, 1, 0, c, :]
                for n in range(HALVES):
                    tok = slice(n * HT, (n + 1) * HT)
                    pe.matmul(out_ps[:, tok], w_hi, h_hi[:, tok], start=True, stop=False)
                    pe.matmul(out_ps[:, tok], w_lo, h_hi[:, tok], start=False, stop=False)
                    last = pe.matmul(out_ps[:, tok], w_hi, h_lo[:, tok], start=False, stop=True)
                last.then_inc(z_ready, 1)

            def layer2(e, c, slot, first):
                pe.wait_ge(hi_ready, C * e + c + 1)
                w_hi, w_lo = ws[:, slot, 0, 1, c, :], ws[:, slot, 1, 1, c, :]
                for n in range(HALVES):
                    tok = slice(n * HT, (n + 1) * HT)
                    if c == 0 and not first:
                        pe.wait_ge(yg_half, HALVES * (e - 1) + n + 1)
                    pe.matmul(yt[:, tok], w_hi, hid_hi[:, c, tok], start=(c == 0), stop=False)
                    pe.matmul(yt[:, tok], w_lo, hid_hi[:, c, tok], start=False, stop=False)
                    if n == 0:
                        pe.wait_ge(lo_ready, C * e + c + 1)
                    last = pe.matmul(yt[:, tok], w_hi, hid_lo[:, c, tok], start=False, stop=(c == C - 1))
                    if c == C - 1:
                        last.then_inc(y_half, 1)
                if c < C - 1:
                    last.then_inc(l2_done, 1)

            def gates_on_all(e, slot, first):
                pe.wait_ge(sel_ready, e + 1)
                if not first:
                    pe.wait_ge(gate_ready, e)
                for n in range(HALVES):
                    tok = slice(n * HT, (n + 1) * HT)
                    last = pe.matmul(aux[:, tok], sel[:, slot, :], gateT[:, tok], start=True, stop=True)
                last.then_inc(gate_ps, 1)

            def gates_transposed():
                pe.wait_ge(parts_ready, 2)
                for b in range(B):
                    last = pe.transpose(aux[0:G16, b * P:(b + 1) * P], gate_parts[:, b, :].bitcast(F32), ident)
                last.then_inc(gateT_ps, 1)

            def second_biases():
                pe.wait_ge(gateT_ready, 1)
                for n in range(HALVES):
                    tok = slice(n * HT, (n + 1) * HT)
                    last = pe.matmul(aux[:, tok], b2_rows[:], gateT[:, tok].bitcast(F32), start=True, stop=True)
                last.then_inc(bias_ps, 1)

            def pair(i, first=False, final=False):
                for k in range(2 * C):
                    e, c = 2 * i + k // C, k % C
                    layer2(e, c, k // C, first and k < C)
                    if first and k == 0:
                        second_biases()
                    if c == 1:
                        if first and k < C:
                            pe.wait_ge(acc_half, HALVES)
                        gates_on_all(e, k // C, first and k < C)
                    if k + LAG < 2 * C or not final:
                        ahead = k + LAG
                        e1, c1 = 2 * i + ahead // C, ahead % C
                        pe.wait_ge(hid_ready, C * e1 + c1 - 1)
                        layer1(e1, c1, (ahead // C) % SLOTS)

            pe.wait_ge(h_hi_ready, HALVES)
            pe.wait_ge(h_lo_ready, HALVES)
            pe.wait_ge(acc_ready, HALVES)
            for c in range(LAG):
                if c >= 2:
                    pe.wait_ge(hid_ready, c - 1)
                layer1(0, c, 0)
            gates_transposed()
            pair(0, first=True)
            with pe.Fori(1, E // 2 - 1) as i:
                pair(i)
            pair(E // 2 - 1, final=True)

        @block.vector
        def _(v):
            count = [0]

            def mark(ins):
                count[0] += 1
                ins.then_inc(dve, 1)
                return count[0]

            def then(ins):
                v.wait_ge(dve, mark(ins))

            def over_batches(grid):
                return grid.unsqueeze(1).broadcast_to((P, BH, P))

            v.wait_ge(gn_in, 16)
            then(v.tensor_scalar(neg_a0[:], gn[:, 1, :], -1.0, None, ALU.mult))

            def operands(n, which):
                hb = slice(n * BH, (n + 1) * BH)
                fv, ftv = f[:, hb, :], ft[:, hb, :]
                rTv = rT[n].rearrange("p (b j) -> p b j", b=BH)
                for m in which:
                    if m == 0:
                        v.wait_ge(f_in[n], 16)
                        v.tensor_tensor(s_b2[:, hb, :], fv, over_batches(gn[:, 0, :]), ALU.mult).then_inc(prod_ready, 1)
                    if m == 1:
                        v.tensor_tensor(u_a0[:, hb, :], fv, over_batches(neg_a0[:]), ALU.mult).then_inc(prod_ready, 1)
                    if m == 2:
                        v.tensor_tensor(u_b0[:, hb, :], fv, over_batches(gn[:, 2, :]), ALU.mult).then_inc(prod_ready, 1)
                    if m == 3:
                        v.wait_ge(gt_in, 16)
                        v.wait_ge(ft_in[n], 16)
                        v.tensor_tensor(u_b1[:, hb, :], ftv, over_batches(gt[:, 0, :]), ALU.mult).then_inc(prod_ready, 1)
                    if m == 4:
                        v.tensor_tensor(u_a1[:, hb, :], ftv, over_batches(gt[:, 1, :]), ALU.mult).then_inc(prod_ready, 1)
                    if m == 5:
                        v.wait_ge(prod_ready, 6 * n + 5)
                        v.wait_ge(rT_ready, n + 1)
                        v.tensor_tensor(wT[:, hb, :], rTv, u_a1[:, hb, :], ALU.subtract).then_inc(prod_ready, 1)

            def advance(n):
                v.wait_ge(dt_in, 16)
                v.wait_ge(df_ready, n + 1)
                for b in range(BH):
                    bb = n * BH + b
                    v.scalar_tensor_tensor(xp[:, bb, :], df[n][:, b * P:(b + 1) * P], dtb[:, bb:bb + 1], f[:, bb, :],
                                           ALU.mult, ALU.add).then_inc(xp_ready, 1)

            def layer_norm(n):
                hb = slice(n * BH, (n + 1) * BH)
                v.wait_ge(xs_ready, n + 1)
                for bb in range(n * BH, (n + 1) * BH):
                    last = mark(v.bn_stats(st1[:, bb, :], xs[:, bb, :]))
                v.wait_ge(dve, last)
                for bb in range(n * BH, (n + 1) * BH):
                    v.bn_aggr(mv1[:, bb, :], st1[:, bb, :]).then_inc(var1_ready, 1)
                v.wait_ge(var1_ready, BH * (n + 1))
                v.wait_ge(sd1_ready, n + 1)
                then(v.reciprocal(rs1[:, hb], sd1[:, hb]))
                for bb in range(n * BH, (n + 1) * BH):
                    v.tensor_scalar(xn[:, bb, :], xs[:, bb, :], mv1[:, bb, 0:1], rs1[:, bb:bb + 1],
                                    ALU.subtract, ALU.mult).then_inc(xn_ready, 1)

            def token_norm(n):
                hb = slice(n * BH, (n + 1) * BH)
                g, b0 = pv[:, LN_G:LN_G + 1], pv[:, LN_B:LN_B + 1]
                if n == 0:
                    v.wait_ge(p128_in, 16)
                    then(v.tensor_scalar(gsq[:], g, g, None, ALU.mult))
                v.wait_ge(xnT_ready, n + 1)
                for b in range(BH):
                    last = mark(v.bn_stats(st2[:, n * BH + b, :], xnT[n][:, b * P:(b + 1) * P]))
                v.wait_ge(dve, last)
                for bb in range(n * BH, (n + 1) * BH):
                    last = mark(v.bn_aggr(mv2[:, bb, :], st2[:, bb, :]))
                v.wait_ge(dve, last)
                v.tensor_scalar(vh[:, hb], mv2[:, hb, 1], gsq[:, 0:1], None, ALU.mult).then_inc(var2_ready, 1)
                then(v.tensor_scalar(mh[:, hb], mv2[:, hb, 0], g, b0, ALU.mult, ALU.add))
                then(v.tensor_scalar(dmean[:, hb], mh[:, hb], -1.0, b0, ALU.mult, ALU.add))
                v.wait_ge(sd2_ready, n + 1)
                then(v.reciprocal(rs2[:, hb], sd2[:, hb]))
                if n == 0:
                    v.wait_ge(gamma_ready, 1)
                    v.wait_ge(net_sb, 6)
                then(v.tensor_tensor(tg[:, hb], rs2[:, hb], gamma[:, hb], ALU.mult))
                mark(v.tensor_scalar(scale[:, hb], tg[:, hb], g, None, ALU.mult))
                then(v.tensor_tensor(shift0[:, hb], dmean[:, hb], tg[:, hb], ALU.mult))
                then(v.tensor_tensor(shift[:, hb], shift0[:, hb], beta[:, hb], ALU.add))
                for b in range(BH):
                    bb = n * BH + b
                    v.tensor_scalar(h[:, bb * P:(bb + 1) * P], xnT[n][:, b * P:(b + 1) * P], scale[:, bb:bb + 1],
                                    shift[:, bb:bb + 1], ALU.mult, ALU.add).then_inc(h_ready, 1)
                tok = slice(n * HT, (n + 1) * HT)
                v.wait_ge(h_ready, BH * (n + 1))
                v.tensor_copy(h_hi[:, tok], h[:, tok]).then_inc(h_hi_ready, 1)
                v.wait_ge(h_hi_ready, n + 1)
                v.tensor_tensor(h_lo[:, tok], h[:, tok], h_hi[:, tok].bitcast(F32), ALU.subtract).then_inc(h_lo_ready, 1)

            def per_expert(t):
                return t[:].unsqueeze(2).broadcast_to((P, B, E))

            def router():
                v.wait_ge(logits_ready, 1)
                lg = small[:, 0:B * E].rearrange("p (b e) -> p b e", e=E)
                ranks = rank[:].unsqueeze(1).broadcast_to((P, B, E))
                then(v.tensor_reduce(lmax[:], lg, AX.X, ALU.max))
                v.tensor_tensor(ld[:], lg, per_expert(lmax), ALU.subtract).then_inc(ld_ready, 1)
                v.wait_ge(exp_ready, 1)
                then(v.tensor_reduce(z[:], pe_[:], AX.X, ALU.add))
                then(v.reciprocal(rz[:], z[:]))
                then(v.tensor_tensor(pr[:], pe_[:], per_expert(rz), ALU.mult))
                then(v.tensor_reduce(m1[:], pr[:], AX.X, ALU.max))
                then(v.tensor_tensor(eq1[:], pr[:], per_expert(m1), ALU.is_equal))
                then(v.tensor_tensor(rk1[:], eq1[:], ranks, ALU.mult))
                then(v.tensor_reduce(rm1[:], rk1[:], AX.X, ALU.max))
                then(v.tensor_tensor(o1[:], rk1[:], per_expert(rm1), ALU.is_equal))
                then(v.scalar_tensor_tensor(rest[:], o1[:], -2.0, pr[:], ALU.mult, ALU.add))
                then(v.tensor_reduce(m2[:], rest[:], AX.X, ALU.max))
                then(v.tensor_tensor(eq2[:], rest[:], per_expert(m2), ALU.is_equal))
                then(v.tensor_tensor(rk2[:], eq2[:], ranks, ALU.mult))
                then(v.tensor_reduce(rm2[:], rk2[:], AX.X, ALU.max))
                then(v.tensor_tensor(o2[:], rk2[:], per_expert(rm2), ALU.is_equal))
                then(v.tensor_tensor(o12[:], o1[:], o2[:], ALU.add))
                then(v.tensor_tensor(pk[:], pr[:], o12[:], ALU.mult))
                then(v.tensor_reduce(ps[:], pk[:], AX.X, ALU.add))
                then(v.reciprocal(rps[:], ps[:]))
                then(v.tensor_tensor(gate[:], pk[:], per_expert(rps), ALU.mult))
                v.tensor_copy(gate_parts[:, :, 0:E], gate[:]).then_inc(parts_ready, 1)
                v.wait_ge(parts_ready, 1)
                v.tensor_tensor(gate_parts[:, :, E:G16], gate[:], gate_parts[:, :, 0:E].bitcast(F32),
                                ALU.subtract).then_inc(parts_ready, 1)

            operands(0, range(6))
            operands(1, (0, 1))
            advance(0)
            operands(1, (2, 3, 4))
            layer_norm(0)
            operands(1, (5,))
            token_norm(0)
            advance(1)
            layer_norm(1)
            token_norm(1)
            v.wait_ge(const_ready, 4)
            router()

            def low_part(e, c, start):
                g = C * e + c
                v.wait_ge(hi_ready, g + 1)
                v.wait_ge(hid_ready, g + 1)
                if not start:
                    if c < C - 1:
                        v.wait_ge(l2_done, (C - 1) * (e - 1) + c + 1)
                    else:
                        v.wait_ge(y_half, HALVES * e)
                v.tensor_tensor(hid_lo[:, c, :], hid[:, c, :], hid_hi[:, c, :].bitcast(F32),
                                ALU.subtract).then_inc(lo_ready, 1)

            def selector(e, slot, first):
                if not first:
                    v.wait_ge(gate_ps, e - 1)
                v.tensor_copy(sel[:, slot, :], sel_all[:, bass.ds(e, 1), :]).then_inc(sel_ready, 1)

            def split_weights(e, slot):
                v.wait_ge(y_half, HALVES * (e - 1))
                src = we[:, bass.ds(e, 1)].rearrange("p o l c m -> p (o l c m)")
                hi = ws[:, slot, 0].rearrange("p l c m -> p (l c m)")
                lo = ws[:, slot, 1].rearrange("p l c m -> p (l c m)")
                v.tensor_copy(hi, src).then_inc(w_hi_ready, 1)
                v.wait_ge(w_hi_ready, e - 1)
                v.tensor_tensor(lo, src, hi.bitcast(F32), ALU.subtract).then_inc(w_ready, 1)

            def first_biases(e, slot, first):
                if not first:
                    v.wait_ge(hid_ready, C * (e - 1))
                v.tensor_copy(b1s[:, slot, :], pv[:, bass.ds(B1_AT + C * e, C)]).then_inc(b1_ready, 1)

            def add_second_biases():
                v.wait_ge(bias_ps, 1)
                v.wait_ge(acc_ready, HALVES)
                for n in range(HALVES):
                    tok = slice(n * HT, (n + 1) * HT)
                    v.tensor_tensor(acc[:, tok], acc[:, tok], aux[:, tok], ALU.add).then_inc(acc_half, 1)

            def add_up(e):
                for n in range(HALVES):
                    tok = slice(n * HT, (n + 1) * HT)
                    v.wait_ge(yg_half, HALVES * e + n + 1)
                    v.wait_ge(acc_half, HALVES * (e + 1))
                    v.tensor_tensor(acc[:, tok], acc[:, tok], yg[:, tok], ALU.add).then_inc(acc_half, 1)

            def gated(e, first):
                v.wait_ge(gate_ready, e + 1)
                if not first:
                    v.wait_ge(acc_half, HALVES * (e + 1))
                for n in range(HALVES):
                    tok = slice(n * HT, (n + 1) * HT)
                    v.wait_ge(y_half, HALVES * e + n + 1)
                    v.tensor_tensor(yg[:, tok], yt[:, tok], gate_all[:, tok], ALU.mult).then_inc(yg_half, 1)

            def pair(i, first=False, final=False):
                for k in range(2):
                    e = 2 * i + k
                    start = first and k == 0
                    low_part(e, 0, start)
                    if start:
                        add_second_biases()
                    else:
                        gated(e - 1, first)
                    low_part(e, 1, start)
                    if not (start or final and k == 1):
                        split_weights(e + 1, (k + 1) % SLOTS)
                    low_part(e, 2, start)
                    if not start:
                        add_up(e - 1)
                    low_part(e, 3, start)
                    if not (final and k == 1):
                        selector(e + 1, (k + 1) % SLOTS, start)
                        first_biases(e + 1, (k + 1) % SLOTS, start)

            v.wait_ge(rows_in, 16 * ROWS_DMAS)
            v.tensor_copy(sel[:, 0, :], sel_all[:, 0, :]).then_inc(sel_ready, 1)
            first_biases(0, 0, True)
            v.wait_ge(w_in[2], 16 * (E - 2))
            pair(0, first=True)
            with v.Fori(1, E // 2 - 1) as i:
                pair(i)
            pair(E // 2 - 1, final=True)
            for n in range(HALVES):
                tok = slice(n * HT, (n + 1) * HT)
                e = E - 1
                if n == 0:
                    v.wait_ge(gate_ready, e + 1)
                    v.wait_ge(acc_half, HALVES * (e + 1))
                v.wait_ge(y_half, HALVES * e + n + 1)
                v.tensor_tensor(yg[:, tok], yt[:, tok], gate_all[:, tok], ALU.mult).then_inc(yg_half, 1)
                v.wait_ge(yg_half, HALVES * e + n + 1)
                v.tensor_tensor(acc[:, tok], acc[:, tok], yg[:, tok], ALU.add).then_inc(acc_half, 1)


def kernel(**inputs):
    import concourse.bacc as bacc
    from concourse.bass_utils import run_bass_kernel_spmd

    given = {name.removeprefix("L0_cond_").removeprefix("L1_cond_"): np.ascontiguousarray(a)
             for name, a in inputs.items()}
    x, a_grid, b_grid = given["x"], given["A_grid"], given["B_grid"]
    mats, selectors = constants()
    first_biases = given["exp_b1"].reshape(E, C, P).transpose(2, 0, 1).reshape(P, E * C)
    p128 = np.concatenate(
        [np.stack([given[n] for n in ("ln_g", "ln_b", "hyp_b1", "hyp_b2")], axis=1), given["sty_b2"].reshape(2, P).T,
         given["router_w"], given["hyp_w2"], given["sty_w1"], first_biases], axis=1)
    emb = np.zeros((SE, SE), np.float32)
    emb[0:NS] = given["subj_emb"]
    p64 = np.concatenate([given["sty_b1"][:, None], given["hyp_w1"], given["sty_w2"], emb], axis=1)
    exp_w = np.stack([given["exp_w1"].reshape(E, P, C, P), given["exp_w2"].reshape(E, C, P, P).transpose(0, 2, 1, 3)],
                     axis=2)
    tensors = {
        "difference_matrices": mats, "expert_selectors": selectors,
        "x": x.transpose(1, 0, 2), "x_exchanged": x.transpose(2, 0, 1),
        "grids": np.stack([b_grid[2], a_grid[0], b_grid[0]], axis=1),
        "grids_exchanged": np.stack([b_grid[1].T, a_grid[1].T], axis=1),
        "dt": given["condB_dt"], "ids": given["itok_B_6_14"],
        "parameters_128": p128, "parameters_64": p64, "exp_w": exp_w, "exp_b2": given["exp_b2"],
    }
    nc = bacc.Bacc("TRN2", target_bir_lowering=False, num_devices=1)
    arrays, args = {}, []
    for name, a in tensors.items():
        arrays[f"in_{name}_dram"] = a = np.ascontiguousarray(a)
        args.append(nc.dram_tensor(f"in_{name}_dram", a.shape, mybir.dt.from_np(a.dtype), kind="ExternalInput").ap())
    out = nc.dram_tensor("out_0_dram", (P, T), F32, kind="ExternalOutput").ap()
    build(nc, *args, out)
    got = run_bass_kernel_spmd(nc, [arrays], core_ids=[0]).results[0]["out_0_dram"]
    return np.ascontiguousarray(got.reshape(P, B, P).transpose(1, 2, 0))
```

```python
from contextlib import ExitStack

import numpy as np

import concourse.bass as bass
from concourse import mybir

F32 = mybir.dt.float32
F32R = mybir.dt.float32r
I32 = mybir.dt.int32
ALU = mybir.AluOpType
ACT = mybir.ActivationFunctionType
AX = mybir.AxisListType

P = 128
B = 8
BH = B // 2
HALVES = 2
HT = BH * P
T = B * P
E = 8
TOPK = 2
FF = 512
C = FF // P
NS = 32
SE = 64
SH = 128
G16 = 2 * E
WARM_START = 9
WARM_STEP = 1
WARM_NORM = 27
WARM_SECOND = 7
GATES_AT = 2
LAG = 3
SLOTS = 2

IDENT, DIFF, HALF_DIFF2 = range(3)
NMAT = 3
LN_G, LN_B, HYP_B1, HYP_B2, STY_BG, STY_BB = range(6)
RW_AT = 6
HW2_AT = RW_AT + E
SW1_AT = HW2_AT + SH
BIAS_AT = SW1_AT + SE
NB = C + 1
N128 = BIAS_AT + E * NB
STY_B1 = 0
HW1_AT = 1
SW2_AT = HW1_AT + SH
EMB_AT = SW2_AT + 2 * P
N64 = EMB_AT + SE


def constants():
    d = np.zeros((P, P), np.float32)
    d2 = np.zeros((P, P), np.float32)
    for m in range(1, P - 1):
        d[m, m + 1], d[m, m - 1] = 0.5, -0.5
        d2[m, m + 1], d2[m, m], d2[m, m - 1] = 1.0, -2.0, 1.0
    d[0, 0:3] = -1.5, 2.0, -0.5
    d[P - 1, P - 3:P] = 0.5, -2.0, 1.5
    d2[0, 0:4] = 2.0, -5.0, 4.0, -1.0
    d2[P - 1, P - 4:P] = -1.0, 4.0, -5.0, 2.0
    mats = np.stack([np.eye(P, dtype=np.float32), d.T, 0.5 * d2.T], axis=1)
    sel = np.zeros((G16, E, P), np.float32)
    for e in range(E):
        sel[e, e] = sel[E + e, e] = 1.0
    return np.ascontiguousarray(mats), sel


def build(nc, const, selectors, x, xT, grids, gridsT, dt, ids, p128, p64, exp_w, out):
    with ExitStack() as ctx:
        def sb(name, shape, dtype=F32):
            return ctx.enter_context(nc.sbuf_tensor(name, shape, dtype))

        def sem(name):
            return ctx.enter_context(nc.semaphore(name))

        mats = sb("mats", [P, NMAT, P])
        sel_all = sb("sel_all", [G16, E, P])
        f = sb("f", [P, B, P])
        ft = sb("ft", [P, B, P])
        gn = sb("gn", [P, 3, P])
        gt = sb("gt", [P, 2, P])
        dtb = sb("dtb", [P, B])
        idi = sb("idi", [NS, B], I32)
        pv = sb("pv", [P, N128])
        pw = sb("pw", [SE, N64])
        we = sb("we", [P, E, 2, C, P])
        warm = sb("warm", [P, HT], mybir.dt.bfloat16)
        table = sb("table", [P, 1])
        neg_a0 = sb("neg_a0", [P, P])
        s_b2 = sb("s_b2", [P, B, P])
        u_a0 = sb("u_a0", [P, B, P])
        u_b0 = sb("u_b0", [P, B, P])
        u_a1 = sb("u_a1", [P, B, P])
        u_b1 = sb("u_b1", [P, B, P])
        wT = sb("wT", [P, B, P])
        xp = sb("xp", [P, B, P])
        xs = sb("xs", [P, B, P])
        st1 = sb("st1", [P, B, 6])
        mv1 = sb("mv1", [P, B, 2])
        sd1 = sb("sd1", [P, B])
        rs1 = sb("rs1", [P, B])
        mrs1 = sb("mrs1", [P, B])
        xn = sb("xn", [P, B, P])
        st2 = sb("st2", [P, B, 6])
        mv2 = sb("mv2", [P, B, 2])
        gsq = sb("gsq", [P, 1])
        vh = sb("vh", [P, B])
        mh = sb("mh", [P, B])
        dmean = sb("dmean", [P, B])
        sd2 = sb("sd2", [P, B])
        rs2 = sb("rs2", [P, B])
        tg = sb("tg", [P, B])
        scale = sb("scale", [P, B])
        shift0 = sb("shift0", [P, B])
        shift = sb("shift", [P, B])
        h = sb("h", [P, T])
        h_hi = sb("h_hi", [P, T], F32R)
        h_lo = sb("h_lo", [P, T], F32R)
        idf = sb("idf", [NS, B])
        idn = sb("idn", [NS, B])
        idw = sb("idw", [NS, B])
        idc = sb("idc", [NS, B])
        row_no = sb("row_no", [NS, 1])
        onehot = sb("onehot", [NS, B])
        se = sb("se", [SE, B])
        hyp1 = sb("hyp1", [SH, B])
        hyp2 = sb("hyp2", [SH, B])
        sty1 = sb("sty1", [SE, B])
        graw = sb("graw", [P, B])
        beta = sb("beta", [P, B])
        gabs = sb("gabs", [P, B])
        gexp = sb("gexp", [P, B])
        glog = sb("glog", [P, B])
        gpos = sb("gpos", [P, B])
        gsum = sb("gsum", [P, B])
        gamma = sb("gamma", [P, B])
        b1s = sb("b1s", [P, SLOTS, NB])
        gneg = sb("gneg", [P, B])
        eps_ln = sb("eps_ln", [P, 1])
        eps_t = sb("eps_t", [P, 1])
        one = sb("one", [P, 1])
        lmax = sb("lmax", [P, B])
        ld = sb("ld", [P, B, E])
        pe_ = sb("pe_", [P, B, E])
        z = sb("z", [P, B])
        rz = sb("rz", [P, B])
        pr = sb("pr", [P, B, E])
        top8 = sb("top8", [P, B, E])
        rest = sb("rest", [P, B, E])
        pk = sb("pk", [P, B, E])
        ps = sb("ps", [P, B])
        rps = sb("rps", [P, B])
        gate = sb("gate", [P, B, E])
        gate_parts = sb("gate_parts", [P, B, G16], F32R)
        gateT = sb("gateT", [G16, T], F32R)
        ws = sb("ws", [P, SLOTS, 2, 2, C, P], F32R)
        sel = sb("sel", [G16, SLOTS, P], F32R)
        hid = sb("hid", [P, C, T])
        hid_hi = sb("hid_hi", [P, C, T], F32R)
        hid_lo = sb("hid_lo", [P, C, T], F32R)
        gate_all = sb("gate_all", [P, T])
        yg = sb("yg", [P, T])
        acc = sb("acc", [P, T])

        zt = [ctx.enter_context(nc.psum_tensor(f"zt{n}", [P, T], F32)) for n in range(2)]
        yt = ctx.enter_context(nc.psum_tensor("yt", [P, T], F32))
        aux = ctx.enter_context(nc.psum_tensor("aux", [P, T], F32))

        def bank(t, n):
            return t[:, n * HT:(n + 1) * HT]

        xsT = bank(aux, 0)
        rT = [bank(zt[1], n) for n in range(HALVES)]
        df = [bank(yt, n) for n in range(HALVES)]

        def xnT(n, b):
            at = (b // 2) * HT + (b % 2) * P
            return (aux, yt)[n][:, at:at + P]

        small = bank(aux, 0)
        lg_ps = bank(aux, 1)
        warm_ps = bank(zt[0], 1)
        ident = mats[:, IDENT, :]

        def per_expert(t):
            return t[:].unsqueeze(2).broadcast_to((P, B, E))

        def over_batches(grid):
            return grid.unsqueeze(1).broadcast_to((P, BH, P))

        mats_in = sem("mats_in")
        f_in = [sem(f"f_in{n}") for n in range(HALVES)]
        ft_in = [sem(f"ft_in{n}") for n in range(HALVES)]
        gn_in = sem("gn_in")
        gt_in = sem("gt_in")
        dt_in = sem("dt_in")
        p128_in = sem("p128_in")
        p64_in = sem("p64_in")
        ids_in = sem("ids_in")
        sel_in = sem("sel_in")
        w_in = [sem(f"w_in{n}") for n in range(3)]
        out_done = sem("out_done")
        pool_chain = sem("pool_chain")
        onehot_ready = sem("onehot_ready")
        const_ready = sem("const_ready")
        gamma_ready = sem("gamma_ready")
        gabs_ready = sem("gabs_ready")
        net_ps = sem("net_ps")
        net_sb = sem("net_sb")
        soft_steps = sem("soft_steps")
        warm_ready = sem("warm_ready")
        s_ready = sem("s_ready")
        a0_ready = sem("a0_ready")
        a1_ready = sem("a1_ready")
        w_op_ready = sem("w_op_ready")
        b_ready = sem("b_ready")
        rT_ready = sem("rT_ready")
        df_ready = sem("df_ready")
        xp_ready = sem("xp_ready")
        xs_ready = sem("xs_ready")
        xs_act_ready = sem("xs_act_ready")
        dve = sem("dve")
        var1_ready = sem("var1_ready")
        sd1_ready = sem("sd1_ready")
        rs1_ready = sem("rs1_ready")
        xn_ready = sem("xn_ready")
        xn_act_ready = sem("xn_act_ready")
        xnT_ready = sem("xnT_ready")
        var2_ready = sem("var2_ready")
        sd2_ready = sem("sd2_ready")
        shift_ready = sem("shift_ready")
        h_ready = sem("h_ready")
        h_act_ready = sem("h_act_ready")
        h_hi_ready = sem("h_hi_ready")
        h_lo_ready = sem("h_lo_ready")
        logits_ready = sem("logits_ready")
        ld_ready = sem("ld_ready")
        exp_ready = sem("exp_ready")
        probs_ready = sem("probs_ready")
        top_sum_ready = sem("top_sum_ready")
        share_ready = sem("share_ready")
        parts_ready = sem("parts_ready")
        gateT_ps = sem("gateT_ps")
        gateT_ready = sem("gateT_ready")
        bias_ps = sem("bias_ps")
        acc_ready = sem("acc_ready")
        w_hi_ready = sem("w_hi_ready")
        w_ready = sem("w_ready")
        b1_ready = sem("b1_ready")
        xsT_ready = sem("xsT_ready")
        sel_ready = sem("sel_ready")
        z_early_ready = sem("z_early_ready")
        hid_early_ready = sem("hid_early_ready")
        z_ready = sem("z_ready")
        hi_ready = sem("hi_ready")
        hid_ready = sem("hid_ready")
        lo_ready = sem("lo_ready")
        l2_done = sem("l2_done")
        y_half = sem("y_half")
        yg_half = sem("yg_half")
        acc_half = sem("acc_half")
        gate_ps = sem("gate_ps")
        gate_ready = sem("gate_ready")

        block = ctx.enter_context(nc.Block())

        @block.sync
        def _(sp):
            def load(tile, source, done):
                sp.dma_start(tile, source).then_inc(done, 16)

            load(gn[:], grids, gn_in)
            load(f[:, 0:BH, :], x[:, 0:BH, :], f_in[0])
            load(gt[:], gridsT, gt_in)
            load(dtb[:], dt.partition_broadcast(P), dt_in)
            load(f[:, BH:B, :], x[:, BH:B, :], f_in[1])
            load(ft[:, BH:B, :], xT[:, BH:B, :], ft_in[1])
            load(we[:, 0], exp_w[0], w_in[0])
            load(sel_all[:], selectors, sel_in)
            for e in range(1, E):
                load(we[:, e], exp_w[e], w_in[min(e, 2)])
            for n in range(HALVES):
                tok = slice(n * HT, (n + 1) * HT)
                sp.wait_ge(acc_half, HALVES * (E - 1) + n + 1)
                sp.dma_start(out[:, tok], acc[:, tok]).then_inc(out_done, 16)
            sp.wait_ge(out_done, 16 * HALVES)

        @block.gpsimd
        def _(pool):
            steps = [0]

            def step(ins):
                steps[0] += 1
                ins.then_inc(pool_chain, 1)
                pool.wait_ge(pool_chain, steps[0])

            pool.dma_start(idi[:], ids.partition_broadcast(NS)).then_inc(ids_in, 16)
            pool.memset(eps_ln[:], 1e-5).then_inc(const_ready, 1)
            pool.memset(eps_t[:], 1e-8).then_inc(const_ready, 1)
            pool.memset(one[:], 1.0).then_inc(const_ready, 1)
            step(pool.iota(row_no[:], pattern=[[0, 1]], base=0, channel_multiplier=1,
                           allow_small_or_imprecise_dtypes=True))
            pool.wait_ge(ids_in, 16)
            step(pool.tensor_copy(idf[:], idi[:]))
            step(pool.tensor_scalar(idn[:], idf[:], 0.0, float(NS), ALU.is_lt, ALU.mult))
            step(pool.tensor_tensor(idw[:], idf[:], idn[:], ALU.add))
            step(pool.tensor_scalar(idc[:], idw[:], float(NS - 1), 0.0, ALU.min, ALU.max))
            pool.tensor_scalar(onehot[:], idc[:], row_no[:, 0:1], None, ALU.is_equal).then_inc(onehot_ready, 1)

            def b_products(n):
                hb = slice(n * BH, (n + 1) * BH)
                pool.wait_ge(f_in[n], 16)
                pool.wait_ge(gn_in, 16)
                pool.tensor_tensor(u_b0[:, hb, :], f[:, hb, :], over_batches(gn[:, 2, :]), ALU.mult).then_inc(b_ready, 1)
                pool.wait_ge(ft_in[n], 16)
                pool.wait_ge(gt_in, 16)
                pool.tensor_tensor(u_b1[:, hb, :], ft[:, hb, :], over_batches(gt[:, 0, :]), ALU.mult).then_inc(b_ready, 1)

            b_products(0)
            b_products(1)
            pool.wait_ge(soft_steps, 2)
            pool.tensor_tensor(gabs[:], gpos[:], gneg[:], ALU.add).then_inc(gabs_ready, 1)
            for e in range(SLOTS):
                pool.wait_ge(w_in[e], 16)
                for layer in range(2):
                    step(pool.tensor_scalar(ws[:, e, 0, layer], we[:, e, layer], 1.0, 0.0, ALU.mult, ALU.add))
                    last = pool.tensor_tensor(ws[:, e, 1, layer], we[:, e, layer], ws[:, e, 0, layer].bitcast(F32),
                                              ALU.subtract)
                    if layer == 0:
                        steps[0] += 1
                        last.then_inc(pool_chain, 1)
                last.then_inc(w_ready, 1)
                pool.wait_ge(pool_chain, steps[0])
                if e == 0:
                    pool.wait_ge(soft_steps, 4)
                    step(pool.tensor_tensor(gsum[:], gpos[:], glog[:], ALU.add))
                    pool.tensor_scalar(gamma[:], gsum[:], 1e-8, None, ALU.add).then_inc(gamma_ready, 1)

        @block.scalar
        def _(act):
            act.dma_start(pw[:], p64).then_inc(p64_in, 16)
            act.dma_start(mats[:], const).then_inc(mats_in, 16)
            act.dma_start(ft[:, 0:BH, :], xT[:, 0:BH, :]).then_inc(ft_in[0], 16)
            act.dma_start(pv[:], p128).then_inc(p128_in, 16)
            act.wait_ge(const_ready, 3)
            act.activation(table[:], one[:], ACT.Exp)
            act.wait_ge(net_ps, 1)
            act.activation(se[:], small[0:SE, 0:B], ACT.Copy).then_inc(net_sb, 1)
            act.wait_ge(p128_in, 16)
            act.wait_ge(p64_in, 16)
            act.wait_ge(net_ps, 2)
            act.activation(hyp1[:], small[:, 0:B], ACT.Relu, bias=pv[:, HYP_B1:HYP_B1 + 1]).then_inc(net_sb, 1)
            act.wait_ge(net_ps, 3)
            act.activation(hyp2[:], small[:, 0:B], ACT.Identity, bias=pv[:, HYP_B2:HYP_B2 + 1]).then_inc(net_sb, 1)
            act.wait_ge(net_ps, 4)
            act.activation(sty1[:], small[0:SE, 0:B], ACT.Relu, bias=pw[:, STY_B1:STY_B1 + 1]).then_inc(net_sb, 1)
            act.wait_ge(net_ps, 5)
            act.activation(graw[:], small[:, 0:B], ACT.Identity, bias=pv[:, STY_BG:STY_BG + 1]).then_inc(net_sb, 1)
            act.activation(beta[:], small[:, B:2 * B], ACT.Identity, bias=pv[:, STY_BB:STY_BB + 1]).then_inc(net_sb, 1)
            act.wait_ge(net_sb, 6)
            act.activation(gpos[:], graw[:], ACT.Relu).then_inc(soft_steps, 1)
            act.activation(gneg[:], graw[:], ACT.Relu, scale=-1.0).then_inc(soft_steps, 1)
            act.wait_ge(gabs_ready, 1)
            act.activation(gexp[:], gabs[:], ACT.Exp, scale=-1.0).then_inc(soft_steps, 1)
            act.wait_ge(soft_steps, 3)
            act.activation(glog[:], gexp[:], ACT.Ln, bias=one[:, 0:1]).then_inc(soft_steps, 1)
            act.activation(table[:], one[:], ACT.Sqrt)

            def relu_step():
                for b in range(BH, B, 2):
                    act.wait_ge(xp_ready, b + 2)
                    act.activation(xs[:, b:b + 2, :], xp[:, b:b + 2, :], ACT.Relu).then_inc(xs_act_ready, 1)

            def sd_features(n):
                act.wait_ge(var1_ready, BH * (n + 1))
                act.activation(sd1[:, n * BH:(n + 1) * BH], mv1[:, n * BH:(n + 1) * BH, 1], ACT.Sqrt,
                               bias=eps_ln[:, 0:1]).then_inc(sd1_ready, 1)

            def normalise(n):
                act.wait_ge(rs1_ready, 2 * (n + 1))
                for b in range(n * BH + 2, (n + 1) * BH):
                    act.activation(xn[:, b, :], xs[:, b, :], ACT.Identity, bias=mrs1[:, b:b + 1],
                                   scale=rs1[:, b:b + 1]).then_inc(xn_act_ready, 1)

            def sd_tokens(n):
                act.wait_ge(var2_ready, n + 1)
                act.activation(sd2[:, n * BH:(n + 1) * BH], vh[:, n * BH:(n + 1) * BH], ACT.Sqrt,
                               bias=eps_t[:, 0:1]).then_inc(sd2_ready, 1)

            def conditioned(n):
                act.wait_ge(shift_ready, 2 * (n + 1))
                for b in range(2, BH):
                    bb = n * BH + b
                    act.activation(h[:, bb * P:(bb + 1) * P], xnT(n, b), ACT.Identity,
                                   bias=shift[:, bb:bb + 1], scale=scale[:, bb:bb + 1]).then_inc(h_act_ready, 1)

            def transposed_step(n):
                act.wait_ge(xsT_ready, n + 1)
                act.activation(acc[:, n * HT:(n + 1) * HT], xsT, ACT.Copy).then_inc(acc_ready, 1)

            def hidden_part(c, n):
                tok = slice(n * HT, (n + 1) * HT)
                if n == 0:
                    act.wait_ge(b1_ready, 1)
                act.wait_ge((z_early_ready, z_ready)[n], c + 1)
                z_ps, bias = zt[c][:, tok], b1s[:, 0, c:c + 1]
                high = act.activation(hid_hi[:, c, tok], z_ps, ACT.Relu, bias=bias)
                whole = act.activation(hid[:, c, tok], z_ps, ACT.Relu, bias=bias)
                if n == 0:
                    whole.then_inc(hid_early_ready, 1)
                else:
                    high.then_inc(hi_ready, 1)
                    whole.then_inc(hid_ready, 1)

            sd_features(0)
            normalise(0)
            relu_step()
            sd_tokens(0)
            sd_features(1)
            conditioned(0)
            normalise(1)
            sd_tokens(1)
            hidden_part(0, 0)
            conditioned(1)
            act.activation(table[:], one[:], ACT.Exp)
            hidden_part(1, 0)
            act.wait_ge(ld_ready, 1)
            act.activation(pe_[:], ld[:], ACT.Exp).then_inc(exp_ready, 1)
            transposed_step(0)

            def hidden(e, c, slot, start):
                g = C * e + c
                act.wait_ge(z_ready, g + 1)
                if not start:
                    if c < C - 1:
                        act.wait_ge(l2_done, (C - 1) * (e - 1) + c + 1)
                    else:
                        act.wait_ge(y_half, HALVES * e)
                bias = b1s[:, slot, c:c + 1]
                if c == 0:
                    act.wait_ge(b1_ready, e + 1)
                act.activation(hid_hi[:, c, :], zt[c % 2][:], ACT.Relu, bias=bias).then_inc(hi_ready, 1)
                if not start:
                    act.wait_ge(lo_ready, g - C + 1)
                act.activation(hid[:, c, :], zt[c % 2][:], ACT.Relu, bias=bias).then_inc(hid_ready, 1)

            def gates_out(e, start):
                act.wait_ge(gate_ps, e + 1)
                if not start:
                    act.wait_ge(yg_half, HALVES * e)
                act.activation(gate_all[:], aux[:], ACT.Copy).then_inc(gate_ready, 1)

            def pair(i, first=False):
                for k in range(2):
                    e = 2 * i + k
                    for c in range(C):
                        if first and k == 0 and c < 2:
                            hidden_part(c, 1)
                        else:
                            hidden(e, c, k, first and k == 0)
                        if first and k == 0 and c == 1:
                            transposed_step(1)
                        if first and k == 0 and c == GATES_AT:
                            act.wait_ge(gateT_ps, 1)
                            act.activation(gateT[:], aux[0:G16, :], ACT.Copy).then_inc(gateT_ready, 1)
                        if c == C - 1:
                            gates_out(e, first and k == 0)

            pair(0, first=True)
            with act.Fori(1, E // 2) as i:
                pair(i)

        @block.tensor
        def _(pe):
            def step_cross(n):
                if n == 0:
                    pe.wait_ge(mats_in, 16)
                pe.wait_ge(s_ready, n + 1)
                for b in range(BH):
                    last = pe.matmul(rT[n][:, b * P:(b + 1) * P], s_b2[:, n * BH + b, :], mats[:, DIFF, :],
                                     start=True, stop=True)
                last.then_inc(rT_ready, 1)

            def step_rows_a(n):
                hb = slice(n * BH, (n + 1) * BH)
                pe.wait_ge(a0_ready, n + 1)
                pe.matmul(df[n], mats[:, DIFF, :], u_a0[:, hb, :].rearrange("p b j -> p (b j)"),
                          start=True, stop=False, skip_group_check=True)

            def step_rows_b(n):
                hb = slice(n * BH, (n + 1) * BH)
                pe.wait_ge(b_ready, 2 * n + 1)
                pe.matmul(df[n], mats[:, HALF_DIFF2, :], u_b0[:, hb, :].rearrange("p b j -> p (b j)"),
                          start=False, stop=False, skip_group_check=True)

            def step_columns_w(n):
                pe.wait_ge(w_op_ready, n + 1)
                for b in range(BH):
                    pe.matmul(df[n][:, b * P:(b + 1) * P], wT[:, n * BH + b, :], mats[:, DIFF, :],
                              start=False, stop=False, skip_group_check=True)

            def step_columns_b(n):
                pe.wait_ge(b_ready, 2 * n + 2)
                for b in range(BH):
                    last = pe.matmul(df[n][:, b * P:(b + 1) * P], u_b1[:, n * BH + b, :], mats[:, HALF_DIFF2, :],
                                     start=False, stop=(b == BH - 1), skip_group_check=True)
                last.then_inc(df_ready, 1)

            def keep_warm(count):
                for _ in range(count):
                    pe.matmul(warm_ps, warm[:, 0:P], warm[:], start=True, stop=True)

            pe.wait_ge(warm_ready, 1)
            keep_warm(WARM_START)
            def net_layer(n, weights, acts, rows):
                pe.matmul(small[0:rows, 0:B], weights, acts, start=True, stop=True).then_inc(net_ps, 1)

            pe.wait_ge(onehot_ready, 1)
            pe.wait_ge(p64_in, 16)
            net_layer(0, pw[0:NS, EMB_AT:EMB_AT + SE], onehot[:], SE)
            keep_warm(WARM_STEP)
            step_cross(0)
            pe.wait_ge(net_sb, 1)
            net_layer(1, pw[:, HW1_AT:HW1_AT + SH], se[:], SH)
            step_rows_a(0)
            pe.wait_ge(p128_in, 16)
            pe.wait_ge(net_sb, 2)
            net_layer(2, pv[:, HW2_AT:HW2_AT + SH], hyp1[:], SH)
            step_rows_b(0)
            pe.wait_ge(net_sb, 3)
            net_layer(3, pv[:, SW1_AT:SW1_AT + SE], hyp2[:], SE)
            step_columns_w(0)
            pe.wait_ge(net_sb, 4)
            pe.matmul(small[:, 0:B], pw[:, SW2_AT:SW2_AT + P], sty1[:], start=True, stop=True)
            pe.matmul(small[:, B:2 * B], pw[:, SW2_AT + P:SW2_AT + 2 * P], sty1[:], start=True,
                      stop=True).then_inc(net_ps, 1)
            step_columns_b(0)
            step_cross(1)
            step_rows_a(1)
            step_rows_b(1)
            step_columns_w(1)
            step_columns_b(1)

            def step_transposed(n):
                if n == 1:
                    pe.wait_ge(acc_ready, 1)
                for b in range(BH):
                    last = pe.transpose(xsT[:, b * P:(b + 1) * P], xs[:, n * BH + b, :], ident)
                last.then_inc(xsT_ready, 1)

            def norm_transposed(n):
                pe.wait_ge(xn_ready, 2 * (n + 1))
                pe.wait_ge(xn_act_ready, 2 * (n + 1))
                if n == 0:
                    pe.wait_ge(net_sb, 6)
                for b in range(BH):
                    last = pe.transpose(xnT(n, b), xn[:, n * BH + b, :], ident)
                last.then_inc(xnT_ready, 1)

            def logits(n):
                pe.wait_ge(h_ready, 2 * (n + 1))
                pe.wait_ge(h_act_ready, 2 * (n + 1))
                for b in range(n * BH, (n + 1) * BH):
                    last = pe.matmul(lg_ps[:, b * E:(b + 1) * E], h[:, b * P:(b + 1) * P], pv[:, RW_AT:RW_AT + E],
                                     start=True, stop=True)
                last.then_inc(logits_ready, 1)

            norm_transposed(0)
            keep_warm(WARM_NORM)
            norm_transposed(1)

            def layer1_half(c, slot, n):
                tok = slice(n * HT, (n + 1) * HT)
                w_hi, w_lo = ws[:, slot, 0, 0, c, :], ws[:, slot, 1, 0, c, :]
                pe.matmul(zt[c % 2][:, tok], w_hi, h_hi[:, tok], start=True, stop=False)
                pe.matmul(zt[c % 2][:, tok], w_lo, h_hi[:, tok], start=False, stop=False)
                return pe.matmul(zt[c % 2][:, tok], w_hi, h_lo[:, tok], start=False, stop=True)

            def layer1(e, c, slot):
                if c == 0:
                    pe.wait_ge(w_ready, e + 1)
                layer1_half(c, slot, 0)
                layer1_half(c, slot, 1).then_inc(z_ready, 1)

            def layer2(e, c, slot, first):
                pe.wait_ge(hi_ready, C * e + c + 1)
                w_hi, w_lo = ws[:, slot, 0, 1, c, :], ws[:, slot, 1, 1, c, :]
                for n in range(HALVES):
                    tok = slice(n * HT, (n + 1) * HT)
                    if c == 0 and not first:
                        pe.wait_ge(yg_half, HALVES * (e - 1) + n + 1)
                    pe.matmul(yt[:, tok], w_hi, hid_hi[:, c, tok], start=(c == 0), stop=False)
                    pe.matmul(yt[:, tok], w_lo, hid_hi[:, c, tok], start=False, stop=False)
                    if n == 0:
                        pe.wait_ge(lo_ready, C * e + c + 1)
                    last = pe.matmul(yt[:, tok], w_hi, hid_lo[:, c, tok], start=False, stop=(c == C - 1))
                    if c == C - 1:
                        last.then_inc(y_half, 1)
                if c < C - 1:
                    last.then_inc(l2_done, 1)

            def gates_on_all(e, slot, first):
                pe.wait_ge(sel_ready, e + 1)
                if not first:
                    pe.wait_ge(gate_ready, e)
                for n in range(HALVES):
                    tok = slice(n * HT, (n + 1) * HT)
                    last = pe.matmul(aux[:, tok], sel[:, slot, :], gateT[:, tok], start=True, stop=True)
                last.then_inc(gate_ps, 1)

            def gates_transposed():
                pe.wait_ge(parts_ready, 1)
                pe.wait_ge(acc_ready, HALVES)
                for b in range(B):
                    last = pe.transpose(aux[0:G16, b * P:(b + 1) * P], gate_parts[:, b, :].bitcast(F32), ident)
                last.then_inc(gateT_ps, 1)

            def pair(i, first=False, final=False):
                for k in range(2 * C):
                    e, c = 2 * i + k // C, k % C
                    layer2(e, c, k // C, first and k < C)
                    start = first and k < C
                    if start and c == GATES_AT - 1:
                        gates_transposed()
                    if c == (GATES_AT if start else 1):
                        if start:
                            pe.wait_ge(gateT_ready, 1)
                        gates_on_all(e, k // C, start)
                    if k + LAG < 2 * C or not final:
                        ahead = k + LAG
                        e1, c1 = 2 * i + ahead // C, ahead % C
                        pe.wait_ge(hid_ready, C * e1 + c1 - 1)
                        layer1(e1, c1, (ahead // C) % SLOTS)

            pe.wait_ge(w_ready, 1)
            for n in range(HALVES):
                pe.wait_ge(h_hi_ready, n + 1)
                pe.wait_ge(h_lo_ready, n + 1)
                for c in range(2):
                    layer1_half(c, 0, n).then_inc((z_early_ready, z_ready)[n], 1)
                if n == 0:
                    logits(0)
                    step_transposed(0)
                    keep_warm(WARM_SECOND)
                    logits(1)
            step_transposed(1)
            pe.wait_ge(hid_ready, 1)
            layer1(0, 2, 0)
            pair(0, first=True)
            with pe.Fori(1, E // 2 - 1) as i:
                pair(i)
            pair(E // 2 - 1, final=True)

        @block.vector
        def _(v):
            count = [0]

            def mark(ins):
                count[0] += 1
                ins.then_inc(dve, 1)
                return count[0]

            def then(ins):
                v.wait_ge(dve, mark(ins))

            v.memset(warm[:], 0.0).then_inc(warm_ready, 1)
            v.wait_ge(gn_in, 16)
            then(v.tensor_scalar(neg_a0[:], gn[:, 1, :], -1.0, None, ALU.mult))

            def operands(n):
                hb = slice(n * BH, (n + 1) * BH)
                v.wait_ge(f_in[n], 16)
                v.tensor_tensor(s_b2[:, hb, :], f[:, hb, :], over_batches(gn[:, 0, :]), ALU.mult).then_inc(s_ready, 1)
                v.tensor_tensor(u_a0[:, hb, :], f[:, hb, :], over_batches(neg_a0[:]), ALU.mult).then_inc(a0_ready, 1)
                v.wait_ge(gt_in, 16)
                v.wait_ge(ft_in[n], 16)
                v.tensor_tensor(u_a1[:, hb, :], ft[:, hb, :], over_batches(gt[:, 1, :]), ALU.mult).then_inc(a1_ready, 1)

            def cross_operand(n):
                hb = slice(n * BH, (n + 1) * BH)
                v.wait_ge(a1_ready, n + 1)
                v.wait_ge(rT_ready, n + 1)
                v.tensor_tensor(wT[:, hb, :], rT[n].rearrange("p (b j) -> p b j", b=BH), u_a1[:, hb, :],
                                ALU.subtract).then_inc(w_op_ready, 1)

            def advance(n):
                v.wait_ge(dt_in, 16)
                v.wait_ge(df_ready, n + 1)
                for b in range(BH):
                    bb = n * BH + b
                    v.scalar_tensor_tensor(xp[:, bb, :], df[n][:, b * P:(b + 1) * P], dtb[:, bb:bb + 1], f[:, bb, :],
                                           ALU.mult, ALU.add).then_inc(xp_ready, 1)

            def feature_stats(n):
                for bb in range(n * BH, (n + 1) * BH):
                    if n == 1:
                        v.wait_ge(xs_act_ready, (bb - BH) // 2 + 1)
                    last = mark(v.bn_stats(st1[:, bb, :], xs[:, bb, :]))
                v.wait_ge(dve, last)
                for bb in range(n * BH, (n + 1) * BH):
                    v.bn_aggr(mv1[:, bb, :], st1[:, bb, :]).then_inc(var1_ready, 1)

            def normalise(n):
                hb = slice(n * BH, (n + 1) * BH)
                v.wait_ge(var1_ready, BH * (n + 1))
                v.wait_ge(sd1_ready, n + 1)
                v.reciprocal(rs1[:, hb], sd1[:, hb]).then_inc(rs1_ready, 1)
                v.wait_ge(rs1_ready, 2 * n + 1)
                v.scalar_tensor_tensor(mrs1[:, hb], mv1[:, hb, 0], -1.0, rs1[:, hb], ALU.mult,
                                       ALU.mult).then_inc(rs1_ready, 1)
                for bb in range(n * BH, n * BH + 2):
                    v.tensor_scalar(xn[:, bb, :], xs[:, bb, :], mv1[:, bb, 0:1], rs1[:, bb:bb + 1],
                                    ALU.subtract, ALU.mult).then_inc(xn_ready, 1)

            def token_stats(n):
                hb = slice(n * BH, (n + 1) * BH)
                g, b0 = pv[:, LN_G:LN_G + 1], pv[:, LN_B:LN_B + 1]
                if n == 0:
                    v.wait_ge(p128_in, 16)
                    then(v.tensor_scalar(gsq[:], g, g, None, ALU.mult))
                v.wait_ge(xnT_ready, n + 1)
                for b in range(BH):
                    last = mark(v.bn_stats(st2[:, n * BH + b, :], xnT(n, b)))
                v.wait_ge(dve, last)
                for bb in range(n * BH, (n + 1) * BH):
                    last = mark(v.bn_aggr(mv2[:, bb, :], st2[:, bb, :]))
                v.wait_ge(dve, last)
                v.tensor_scalar(vh[:, hb], mv2[:, hb, 1], gsq[:, 0:1], None, ALU.mult).then_inc(var2_ready, 1)
                then(v.tensor_scalar(mh[:, hb], mv2[:, hb, 0], g, b0, ALU.mult, ALU.add))
                then(v.tensor_scalar(dmean[:, hb], mh[:, hb], -1.0, b0, ALU.mult, ALU.add))

            def scale_and_shift(n):
                hb = slice(n * BH, (n + 1) * BH)
                g = pv[:, LN_G:LN_G + 1]
                v.wait_ge(sd2_ready, n + 1)
                then(v.reciprocal(rs2[:, hb], sd2[:, hb]))
                if n == 0:
                    v.wait_ge(gamma_ready, 1)
                    v.wait_ge(net_sb, 6)
                then(v.tensor_tensor(tg[:, hb], rs2[:, hb], gamma[:, hb], ALU.mult))
                then(v.tensor_tensor(shift0[:, hb], dmean[:, hb], tg[:, hb], ALU.mult))
                v.tensor_scalar(scale[:, hb], tg[:, hb], g, None, ALU.mult).then_inc(shift_ready, 1)
                v.tensor_tensor(shift[:, hb], shift0[:, hb], beta[:, hb], ALU.add).then_inc(shift_ready, 1)

            def conditioned(n):
                v.wait_ge(shift_ready, 2 * (n + 1))
                for b in range(2):
                    bb = n * BH + b
                    v.tensor_scalar(h[:, bb * P:(bb + 1) * P], xnT(n, b), scale[:, bb:bb + 1], shift[:, bb:bb + 1],
                                    ALU.mult, ALU.add).then_inc(h_ready, 1)

            def input_parts(n):
                tok = slice(n * HT, (n + 1) * HT)
                v.wait_ge(h_ready, 2 * (n + 1))
                v.wait_ge(h_act_ready, 2 * (n + 1))
                v.tensor_copy(h_hi[:, tok], h[:, tok]).then_inc(h_hi_ready, 1)
                v.wait_ge(h_hi_ready, n + 1)
                v.tensor_tensor(h_lo[:, tok], h[:, tok], h_hi[:, tok].bitcast(F32), ALU.subtract).then_inc(h_lo_ready, 1)

            def router_start():
                v.wait_ge(logits_ready, HALVES)
                lg = lg_ps[:, 0:B * E].rearrange("p (b e) -> p b e", e=E)
                then(v.tensor_reduce(lmax[:], lg, AX.X, ALU.max))
                v.tensor_tensor(ld[:], lg, per_expert(lmax), ALU.subtract).then_inc(ld_ready, 1)

            def router():
                v.wait_ge(exp_ready, 1)
                then(v.tensor_reduce(z[:], pe_[:], AX.X, ALU.add))
                then(v.reciprocal(rz[:], z[:]))
                then(v.tensor_tensor(pr[:], pe_[:], per_expert(rz), ALU.mult))
                for b in range(B):
                    last = mark(v.max(top8[:, b, :], pr[:, b, :]))
                v.wait_ge(dve, last)
                then(v.tensor_tensor(ps[:], top8[:, :, 0], top8[:, :, 1], ALU.add))
                mark(v.reciprocal(rps[:], ps[:]))
                then(v.memset(top8[:, :, TOPK:E], -1.0))
                for b in range(B):
                    last = mark(v.match_replace(rest[:, b, :], top8[:, b, :], pr[:, b, :], 0.0))
                v.wait_ge(dve, last)
                then(v.tensor_tensor(pk[:], pr[:], rest[:], ALU.subtract))
                then(v.tensor_tensor(gate[:], pk[:], per_expert(rps), ALU.mult))
                then(v.tensor_copy(gate_parts[:, :, 0:E], gate[:]))
                v.tensor_tensor(gate_parts[:, :, E:G16], gate[:], gate_parts[:, :, 0:E].bitcast(F32),
                                ALU.subtract).then_inc(parts_ready, 1)

            operands(0)
            cross_operand(0)
            operands(1)
            v.wait_ge(p128_in, 16)
            v.tensor_copy(b1s[:, 0, :], pv[:, BIAS_AT:BIAS_AT + NB]).then_inc(b1_ready, 1)
            v.wait_ge(sel_in, 16)
            v.tensor_copy(sel[:, 0, :], sel_all[:, 0, :]).then_inc(sel_ready, 1)
            advance(0)
            cross_operand(1)
            v.wait_ge(xp_ready, BH)
            v.tensor_scalar(xs[:, 0:BH, :], xp[:, 0:BH, :], 0.0, None, ALU.max).then_inc(xs_ready, 1)
            v.wait_ge(xs_ready, 1)
            feature_stats(0)
            normalise(0)
            advance(1)
            token_stats(0)
            feature_stats(1)
            scale_and_shift(0)
            conditioned(0)
            normalise(1)
            input_parts(0)
            token_stats(1)
            scale_and_shift(1)
            conditioned(1)
            input_parts(1)
            router_start()
            for c in range(2):
                v.wait_ge(hid_early_ready, c + 1)
                v.tensor_tensor(hid_lo[:, c, 0:HT], hid[:, c, 0:HT], hid_hi[:, c, 0:HT].bitcast(F32), ALU.subtract)

            def low_part(e, c, start):
                g = C * e + c
                v.wait_ge(hi_ready, g + 1)
                v.wait_ge(hid_ready, g + 1)
                if start and c < 2:
                    v.tensor_tensor(hid_lo[:, c, HT:T], hid[:, c, HT:T], hid_hi[:, c, HT:T].bitcast(F32),
                                    ALU.subtract).then_inc(lo_ready, 1)
                    return
                if not start:
                    if c < C - 1:
                        v.wait_ge(l2_done, (C - 1) * (e - 1) + c + 1)
                    else:
                        v.wait_ge(y_half, HALVES * e)
                v.tensor_tensor(hid_lo[:, c, :], hid[:, c, :], hid_hi[:, c, :].bitcast(F32),
                                ALU.subtract).then_inc(lo_ready, 1)

            def selector(e, slot, first):
                if not first:
                    v.wait_ge(gate_ps, e - 1)
                v.tensor_copy(sel[:, slot, :], sel_all[:, bass.ds(e, 1), :]).then_inc(sel_ready, 1)

            def split_weights(e, slot):
                v.wait_ge(y_half, HALVES * (e - 1))
                src = we[:, bass.ds(e, 1)].rearrange("p o l c m -> p (o l c m)")
                hi = ws[:, slot, 0].rearrange("p l c m -> p (l c m)")
                lo = ws[:, slot, 1].rearrange("p l c m -> p (l c m)")
                v.tensor_copy(hi, src).then_inc(w_hi_ready, 1)
                v.wait_ge(w_hi_ready, e - 1)
                v.tensor_tensor(lo, src, hi.bitcast(F32), ALU.subtract).then_inc(w_ready, 1)

            def biases(e, slot, first):
                if not first:
                    v.wait_ge(hid_ready, C * (e - 1))
                    v.wait_ge(yg_half, HALVES * (e - 1))
                v.tensor_copy(b1s[:, slot, :], pv[:, bass.ds(BIAS_AT + NB * e, NB)]).then_inc(b1_ready, 1)

            def add_up(e, first):
                for n in range(HALVES):
                    tok = slice(n * HT, (n + 1) * HT)
                    v.wait_ge(yg_half, HALVES * e + n + 1)
                    if first:
                        v.wait_ge(acc_ready, HALVES)
                    else:
                        v.wait_ge(acc_half, HALVES * e)
                    v.tensor_tensor(acc[:, tok], acc[:, tok], yg[:, tok], ALU.add).then_inc(acc_half, 1)

            def gated(e, slot, first):
                v.wait_ge(gate_ready, e + 1)
                if not first:
                    v.wait_ge(acc_half, HALVES * e)
                for n in range(HALVES):
                    tok = slice(n * HT, (n + 1) * HT)
                    v.wait_ge(y_half, HALVES * e + n + 1)
                    v.scalar_tensor_tensor(yg[:, tok], yt[:, tok], b1s[:, slot, C:NB], gate_all[:, tok], ALU.add,
                                           ALU.mult).then_inc(yg_half, 1)

            def pair(i, first=False, final=False):
                for k in range(2):
                    e = 2 * i + k
                    start = first and k == 0
                    low_part(e, 0, start)
                    if not start:
                        gated(e - 1, (k + 1) % SLOTS, first)
                    low_part(e, 1, start)
                    if start:
                        router()
                    if not (final and k == 1):
                        biases(e + 1, (k + 1) % SLOTS, start)
                        selector(e + 1, (k + 1) % SLOTS, start)
                        if not start:
                            split_weights(e + 1, (k + 1) % SLOTS)
                    low_part(e, 2, start)
                    if not start:
                        add_up(e - 1, first)
                    low_part(e, 3, start)

            v.wait_ge(w_in[2], 16 * (E - 2))
            pair(0, first=True)
            with v.Fori(1, E // 2 - 1) as i:
                pair(i)
            pair(E // 2 - 1, final=True)
            for n in range(HALVES):
                tok = slice(n * HT, (n + 1) * HT)
                e, slot = E - 1, (E - 1) % SLOTS
                if n == 0:
                    v.wait_ge(gate_ready, e + 1)
                    v.wait_ge(acc_half, HALVES * e)
                v.wait_ge(y_half, HALVES * e + n + 1)
                v.scalar_tensor_tensor(yg[:, tok], yt[:, tok], b1s[:, slot, C:NB], gate_all[:, tok], ALU.add,
                                           ALU.mult).then_inc(yg_half, 1)
                v.wait_ge(yg_half, HALVES * e + n + 1)
                v.tensor_tensor(acc[:, tok], acc[:, tok], yg[:, tok], ALU.add).then_inc(acc_half, 1)


def kernel(**inputs):
    import concourse.bacc as bacc
    from concourse.bass_utils import run_bass_kernel_spmd

    given = {name.removeprefix("L0_cond_").removeprefix("L1_cond_"): np.ascontiguousarray(a)
             for name, a in inputs.items()}
    x, a_grid, b_grid = given["x"], given["A_grid"], given["B_grid"]
    mats, selectors = constants()
    expert_biases = np.concatenate([given["exp_b1"].reshape(E, C, P), given["exp_b2"][:, None, :]], axis=1)
    expert_biases = expert_biases.transpose(2, 0, 1).reshape(P, E * NB)
    p128 = np.concatenate(
        [np.stack([given[n] for n in ("ln_g", "ln_b", "hyp_b1", "hyp_b2")], axis=1), given["sty_b2"].reshape(2, P).T,
         given["router_w"], given["hyp_w2"], given["sty_w1"], expert_biases], axis=1)
    emb = np.zeros((SE, SE), np.float32)
    emb[0:NS] = given["subj_emb"]
    p64 = np.concatenate([given["sty_b1"][:, None], given["hyp_w1"], given["sty_w2"], emb], axis=1)
    exp_w = np.stack([given["exp_w1"].reshape(E, P, C, P), given["exp_w2"].reshape(E, C, P, P).transpose(0, 2, 1, 3)],
                     axis=2)
    tensors = {
        "difference_matrices": mats, "expert_selectors": selectors,
        "x": x.transpose(1, 0, 2), "x_exchanged": x.transpose(2, 0, 1),
        "grids": np.stack([b_grid[2], a_grid[0], b_grid[0]], axis=1),
        "grids_exchanged": np.stack([b_grid[1].T, a_grid[1].T], axis=1),
        "dt": given["condB_dt"], "ids": given["itok_B_6_14"],
        "parameters_128": p128, "parameters_64": p64, "exp_w": exp_w,
    }
    nc = bacc.Bacc("TRN2", target_bir_lowering=False, num_devices=1)
    arrays, args = {}, []
    for name, a in tensors.items():
        arrays[f"in_{name}_dram"] = a = np.ascontiguousarray(a)
        args.append(nc.dram_tensor(f"in_{name}_dram", a.shape, mybir.dt.from_np(a.dtype), kind="ExternalInput").ap())
    out = nc.dram_tensor("out_0_dram", (P, T), F32, kind="ExternalOutput").ap()
    build(nc, *args, out)
    got = run_bass_kernel_spmd(nc, [arrays], core_ids=[0]).results[0]["out_0_dram"]
    return np.ascontiguousarray(got.reshape(P, B, P).transpose(1, 2, 0))
```

```python
from contextlib import ExitStack

import numpy as np

import concourse.bass as bass
from concourse import mybir

F32 = mybir.dt.float32
F32R = mybir.dt.float32r
I32 = mybir.dt.int32
ALU = mybir.AluOpType
ACT = mybir.ActivationFunctionType
AX = mybir.AxisListType

P = 128
B = 8
BH = B // 2
HALVES = 2
HT = BH * P
T = B * P
E = 8
TOPK = 2
FF = 512
C = FF // P
NS = 32
SE = 64
SH = 128
WARM_START = 8
WARM_NORM = 16
WARM_HALF = 4
XN_DVE = (2, 3)
H_DVE = (2, 2)
GATES_AT = 1
LAG = 3
SLOTS = 2

IDENT, HALF_DIFF2 = range(2)
NMAT = 2
LN_G, LN_B, HYP_B1, HYP_B2, STY_BG, STY_BB = range(6)
RW_AT = 6
HW2_AT = RW_AT + E
SW1_AT = HW2_AT + SH
BIAS_AT = SW1_AT + SE
NB = C + 1
N128 = BIAS_AT + E * NB
STY_B1 = 0
HW1_AT = 1
SW2_AT = HW1_AT + SH
EMB_AT = SW2_AT + 2 * P
N64 = EMB_AT + SE


def constants():
    d = np.zeros((P, P), np.float32)
    d2 = np.zeros((P, P), np.float32)
    for m in range(1, P - 1):
        d[m, m + 1], d[m, m - 1] = 0.5, -0.5
        d2[m, m + 1], d2[m, m], d2[m, m - 1] = 1.0, -2.0, 1.0
    d[0, 0:3] = -1.5, 2.0, -0.5
    d[P - 1, P - 3:P] = 0.5, -2.0, 1.5
    d2[0, 0:4] = 2.0, -5.0, 4.0, -1.0
    d2[P - 1, P - 4:P] = -1.0, 4.0, -5.0, 2.0
    return d.T, np.stack([np.eye(P, dtype=np.float32), 0.5 * d2.T], axis=1)


def build(nc, first_operands, const, x, xT, grids, gridsT, dt, ids, p128, p64, exp_w, out):
    with ExitStack() as ctx:
        def sb(name, shape, dtype=F32):
            return ctx.enter_context(nc.sbuf_tensor(name, shape, dtype))

        def sem(name):
            return ctx.enter_context(nc.semaphore(name))

        mats = sb("mats", [P, NMAT, P])
        f = sb("f", [P, B, P])
        ft = sb("ft", [P, B, P])
        first = sb("first", [P, 2, P])
        gn = sb("gn", [P, 2, P])
        gt = sb("gt", [P, 2, P])
        dtb = sb("dtb", [P, B])
        idi = sb("idi", [NS, B], I32)
        pv = sb("pv", [P, N128])
        pw = sb("pw", [SE, N64])
        we = sb("we", [P, E, 2, C, P])
        warm = sb("warm", [P, HT], mybir.dt.bfloat16)
        table = sb("table", [P, 1])
        neg_a0 = sb("neg_a0", [P, P])
        s_b2 = sb("s_b2", [P, B, P])
        u_a0 = sb("u_a0", [P, B, P])
        u_b0 = sb("u_b0", [P, B, P])
        u_a1 = sb("u_a1", [P, B, P])
        diffs = sb("diffs", [P, 2, P], F32R)
        rows_hi = sb("rows_hi", [P, 2, BH, P], F32R)
        rows_lo = sb("rows_lo", [P, 2, BH, P], F32R)
        u_b1 = sb("u_b1", [P, B, P])
        wT = sb("wT", [P, B, P])
        xp = sb("xp", [P, B, P])
        xs = sb("xs", [P, B, P])
        st1 = sb("st1", [P, B, 6])
        mv1 = sb("mv1", [P, B, 2])
        sd1 = sb("sd1", [P, B])
        rs1 = sb("rs1", [P, B])
        mrs1 = sb("mrs1", [P, B])
        xn = sb("xn", [P, B, P])
        st2 = sb("st2", [P, B, 6])
        mv2 = sb("mv2", [P, B, 2])
        gsq = sb("gsq", [P, 1])
        vh = sb("vh", [P, B])
        mh = sb("mh", [P, B])
        dmean = sb("dmean", [P, B])
        sd2 = sb("sd2", [P, B])
        rs2 = sb("rs2", [P, B])
        tg = sb("tg", [P, B])
        scale = sb("scale", [P, B])
        shift0 = sb("shift0", [P, B])
        shift = sb("shift", [P, B])
        h = sb("h", [P, T])
        h_hi = sb("h_hi", [P, T], F32R)
        h_lo = sb("h_lo", [P, T], F32R)
        idf = sb("idf", [NS, B])
        idn = sb("idn", [NS, B])
        idw = sb("idw", [NS, B])
        idc = sb("idc", [NS, B])
        row_no = sb("row_no", [NS, 1])
        onehot = sb("onehot", [NS, B])
        se = sb("se", [SE, B])
        hyp1 = sb("hyp1", [SH, B])
        hyp2 = sb("hyp2", [SH, B])
        sty1 = sb("sty1", [SE, B])
        graw = sb("graw", [P, B])
        beta = sb("beta", [P, B])
        gabs = sb("gabs", [P, B])
        gexp = sb("gexp", [P, B])
        glog = sb("glog", [P, B])
        gpos = sb("gpos", [P, B])
        gsum = sb("gsum", [P, B])
        gamma = sb("gamma", [P, B])
        gamma_g = sb("gamma_g", [P, B])
        b1s = sb("b1s", [P, SLOTS, NB])
        gneg = sb("gneg", [P, B])
        eps_ln = sb("eps_ln", [P, 1])
        eps_t = sb("eps_t", [P, 1])
        one = sb("one", [P, 1])
        lmax = sb("lmax", [P, B])
        ld = sb("ld", [P, B, E])
        pe_ = sb("pe_", [P, B, E])
        z = sb("z", [P, B])
        rz = sb("rz", [P, B])
        pr = sb("pr", [P, B, E])
        top8 = sb("top8", [P, B, E])
        rest = sb("rest", [P, B, E])
        pk = sb("pk", [P, B, E])
        ps = sb("ps", [P, B])
        rps = sb("rps", [P, B])
        gate = sb("gate", [P, B, E])
        gateT = sb("gateT", [E, T])
        ws = sb("ws", [P, SLOTS, 2, 2, C, P], F32R)
        hid = sb("hid", [P, C, T])
        hid_hi = sb("hid_hi", [P, C, T], F32R)
        hid_lo = sb("hid_lo", [P, C, T], F32R)
        gate_all = sb("gate_all", [P, SLOTS, T])
        yg = sb("yg", [P, T])
        acc = sb("acc", [P, T])

        zt = [ctx.enter_context(nc.psum_tensor(f"zt{n}", [P, T], F32)) for n in range(2)]
        yt = ctx.enter_context(nc.psum_tensor("yt", [P, T], F32))
        aux = ctx.enter_context(nc.psum_tensor("aux", [P, T], F32))

        def bank(t, n):
            return t[:, n * HT:(n + 1) * HT]

        xsT = [bank(zt[1], n) for n in range(HALVES)]
        rT = [bank(zt[1], n) for n in range(HALVES)]
        df = [bank(yt, n) for n in range(HALVES)]

        def xnT(n, b):
            at = (b // 2) * HT + (b % 2) * P
            return (aux, yt)[n][:, at:at + P]

        small = bank(aux, 0)
        lg_ps = bank(aux, 1)
        warm_ps = bank(zt[0], 1)
        y_halves = [(bank(yt, n), slice(n * HT, (n + 1) * HT)) for n in range(HALVES)]
        y_last = [y_halves[0], (yt[:, HT:HT + 2 * P], slice(HT, HT + 2 * P)), (aux[:, 0:2 * P], slice(HT + 2 * P, T))]
        ident = mats[:, IDENT, :]
        b2_grid, diff = first[:, 0, :], first[:, 1, :]

        def per_expert(t):
            return t[:].unsqueeze(2).broadcast_to((P, B, E))

        def over_batches(grid):
            return grid.unsqueeze(1).broadcast_to((P, BH, P))

        mats_in = sem("mats_in")
        f_in = [sem(f"f_in{n}") for n in range(HALVES)]
        ft_in = [sem(f"ft_in{n}") for n in range(HALVES)]
        first_in = sem("first_in")
        gn_in = sem("gn_in")
        gt_in = sem("gt_in")
        dt_in = sem("dt_in")
        p128_in = sem("p128_in")
        p64_in = sem("p64_in")
        ids_in = sem("ids_in")
        w_in = [sem(f"w_in{n}") for n in range(3)]
        out_done = sem("out_done")
        pool_chain = sem("pool_chain")
        onehot_ready = sem("onehot_ready")
        const_ready = sem("const_ready")
        gamma_ready = sem("gamma_ready")
        gabs_ready = sem("gabs_ready")
        net_ps = sem("net_ps")
        net_sb = sem("net_sb")
        soft_steps = sem("soft_steps")
        warm_ready = sem("warm_ready")
        s_ready = sem("s_ready")
        a0_ready = sem("a0_ready")
        a1_ready = sem("a1_ready")
        w_op_ready = sem("w_op_ready")
        diffs_ready = sem("diffs_ready")
        rows_hi_ready = sem("rows_hi_ready")
        rows_lo_ready = sem("rows_lo_ready")
        b_ready = sem("b_ready")
        rT_ready = sem("rT_ready")
        df_ready = sem("df_ready")
        xp_ready = sem("xp_ready")
        xs_ready = sem("xs_ready")
        xs_act_ready = sem("xs_act_ready")
        dve = sem("dve")
        var1_ready = sem("var1_ready")
        sd1_ready = sem("sd1_ready")
        rs1_ready = sem("rs1_ready")
        xn_ready = sem("xn_ready")
        xn_act_ready = sem("xn_act_ready")
        xnT_ready = sem("xnT_ready")
        var2_ready = sem("var2_ready")
        sd2_ready = sem("sd2_ready")
        shift_ready = sem("shift_ready")
        h_ready = sem("h_ready")
        h_act_ready = sem("h_act_ready")
        h_hi_ready = [sem(f"h_hi_ready{n}") for n in range(HALVES)]
        h_lo_ready = [sem(f"h_lo_ready{n}") for n in range(HALVES)]
        logits_ready = sem("logits_ready")
        ld_ready = sem("ld_ready")
        exp_ready = sem("exp_ready")
        gates_ready = sem("gates_ready")
        gateT_ps = sem("gateT_ps")
        gateT_ready = sem("gateT_ready")
        acc_ready = sem("acc_ready")
        w_hi_ready = sem("w_hi_ready")
        w_ready = sem("w_ready")
        b1_ready = sem("b1_ready")
        xsT_ready = sem("xsT_ready")
        z_early_ready = sem("z_early_ready")
        hid_early_ready = sem("hid_early_ready")
        lo_early_ready = sem("lo_early_ready")
        z_ready = sem("z_ready")
        hi_ready = sem("hi_ready")
        hid_ready = sem("hid_ready")
        lo_ready = sem("lo_ready")
        z_last_ready = sem("z_last_ready")
        l2_done = sem("l2_done")
        y_last_ready = sem("y_last_ready")
        yg_last_ready = sem("yg_last_ready")
        out_ready = [sem(f"out_ready{n}") for n in range(3)]
        y_half = sem("y_half")
        yg_half = sem("yg_half")
        acc_half = sem("acc_half")
        gate_ready = [sem(f"gate_ready{n}") for n in range(SLOTS)]

        block = ctx.enter_context(nc.Block())

        @block.sync
        def _(sp):
            def load(tile, source, done):
                sp.dma_start(tile, source).then_inc(done, 16)

            load(f[:, 0:BH, :], x[:, 0:BH, :], f_in[0])
            load(gn[:], grids, gn_in)
            load(ft[:, 0:BH, :], xT[:, 0:BH, :], ft_in[0])
            load(mats[:], const, mats_in)
            load(pv[:], p128, p128_in)
            load(f[:, BH:B, :], x[:, BH:B, :], f_in[1])
            load(ft[:, BH:B, :], xT[:, BH:B, :], ft_in[1])
            load(dtb[:], dt.partition_broadcast(P), dt_in)
            load(we[:, 0], exp_w[0], w_in[0])
            for e in range(1, E):
                load(we[:, e], exp_w[e], w_in[min(e, 2)])
            sp.wait_ge(gateT_ready, 1)
            for e in range(E):
                if e >= SLOTS:
                    sp.wait_ge(yg_half, HALVES * (e - SLOTS + 1))
                row = gateT[e:e + 1, :].unsqueeze(1).broadcast_to((1, P, T))
                sp.dma_start(gate_all[:, e % SLOTS, :], row).then_inc(gate_ready[e % SLOTS], 16)
            for p, (_, tok) in enumerate(y_last):
                sp.wait_ge(out_ready[p], 1)
                sp.dma_start(out[:, tok], acc[:, tok]).then_inc(out_done, 16)
            sp.wait_ge(out_done, 16 * len(y_last))

        @block.gpsimd
        def _(pool):
            steps = [0]

            def step(ins):
                steps[0] += 1
                ins.then_inc(pool_chain, 1)
                pool.wait_ge(pool_chain, steps[0])

            pool.dma_start(idi[:], ids.partition_broadcast(NS)).then_inc(ids_in, 16)
            step(pool.iota(row_no[:], pattern=[[0, 1]], base=0, channel_multiplier=1,
                           allow_small_or_imprecise_dtypes=True))
            pool.wait_ge(ids_in, 16)
            step(pool.tensor_copy(idf[:], idi[:]))
            step(pool.tensor_scalar(idn[:], idf[:], 0.0, float(NS), ALU.is_lt, ALU.mult))
            step(pool.tensor_tensor(idw[:], idf[:], idn[:], ALU.add))
            step(pool.tensor_scalar(idc[:], idw[:], float(NS - 1), 0.0, ALU.min, ALU.max))
            pool.tensor_scalar(onehot[:], idc[:], row_no[:, 0:1], None, ALU.is_equal).then_inc(onehot_ready, 1)

            def b_products(n):
                hb = slice(n * BH, (n + 1) * BH)
                pool.wait_ge(f_in[n], 16)
                pool.wait_ge(gn_in, 16)
                pool.tensor_tensor(u_b0[:, hb, :], f[:, hb, :], over_batches(gn[:, 1, :]),
                                   ALU.mult).then_inc(b_ready, 1)
                pool.wait_ge(ft_in[n], 16)
                pool.wait_ge(gt_in, 16)
                pool.tensor_tensor(u_b1[:, hb, :], ft[:, hb, :], over_batches(gt[:, 0, :]),
                                   ALU.mult).then_inc(b_ready, 1)

            b_products(0)
            b_products(1)
            pool.wait_ge(soft_steps, 2)
            pool.tensor_tensor(gabs[:], gpos[:], gneg[:], ALU.add).then_inc(gabs_ready, 1)
            for e in range(SLOTS):
                pool.wait_ge(w_in[e], 16)
                for layer in range(2):
                    step(pool.tensor_scalar(ws[:, e, 0, layer], we[:, e, layer], 1.0, 0.0, ALU.mult, ALU.add))
                    last = pool.tensor_tensor(ws[:, e, 1, layer], we[:, e, layer], ws[:, e, 0, layer].bitcast(F32),
                                              ALU.subtract)
                    if layer == 0:
                        steps[0] += 1
                        last.then_inc(pool_chain, 1)
                last.then_inc(w_ready, 1)
                pool.wait_ge(pool_chain, steps[0])
                if e == 0:
                    pool.wait_ge(soft_steps, 4)
                    step(pool.tensor_tensor(gsum[:], gpos[:], glog[:], ALU.add))
                    pool.tensor_scalar(gamma[:], gsum[:], 1e-8, None, ALU.add).then_inc(gamma_ready, 1)
                    pool.wait_ge(gamma_ready, 1)
                    pool.wait_ge(p128_in, 16)
                    pool.tensor_scalar(gamma_g[:], gamma[:], pv[:, LN_G:LN_G + 1], None,
                                       ALU.mult).then_inc(gamma_ready, 1)
            pool.wait_ge(h_hi_ready[0], 1)
            pool.tensor_tensor(h_lo[:, 0:HT], h[:, 0:HT], h_hi[:, 0:HT].bitcast(F32),
                               ALU.subtract).then_inc(h_lo_ready[0], 1)
            tok = y_last[0][1]
            pool.wait_ge(yg_last_ready, 1)
            pool.wait_ge(acc_half, HALVES * (E - 1))
            pool.tensor_tensor(acc[:, tok], acc[:, tok], yg[:, tok], ALU.add).then_inc(out_ready[0], 1)

        @block.scalar
        def _(act):
            act.dma_start(first[:], first_operands).then_inc(first_in, 16)
            act.dma_start(pw[:], p64).then_inc(p64_in, 16)
            act.dma_start(gt[:], gridsT).then_inc(gt_in, 16)
            act.wait_ge(const_ready, 3)
            act.activation(table[:], one[:], ACT.Exp)

            def row_high_parts(m):
                act.wait_ge((a0_ready, b_ready)[m], 1)
                act.activation(rows_hi[:, m], (u_a0, u_b0)[m][:, 0:BH, :], ACT.Copy).then_inc(rows_hi_ready, 1)

            row_high_parts(0)
            act.wait_ge(net_ps, 1)
            act.activation(se[:], small[0:SE, 0:B], ACT.Copy).then_inc(net_sb, 1)
            row_high_parts(1)
            act.wait_ge(p128_in, 16)
            act.wait_ge(p64_in, 16)
            act.wait_ge(net_ps, 2)
            act.activation(hyp1[:], small[:, 0:B], ACT.Relu, bias=pv[:, HYP_B1:HYP_B1 + 1]).then_inc(net_sb, 1)
            act.wait_ge(net_ps, 3)
            act.activation(hyp2[:], small[:, 0:B], ACT.Identity, bias=pv[:, HYP_B2:HYP_B2 + 1]).then_inc(net_sb, 1)
            act.wait_ge(net_ps, 4)
            act.activation(sty1[:], small[0:SE, 0:B], ACT.Relu, bias=pw[:, STY_B1:STY_B1 + 1]).then_inc(net_sb, 1)
            act.wait_ge(net_ps, 5)
            act.activation(graw[:], small[:, 0:B], ACT.Identity, bias=pv[:, STY_BG:STY_BG + 1]).then_inc(net_sb, 1)
            act.activation(beta[:], small[:, B:2 * B], ACT.Identity, bias=pv[:, STY_BB:STY_BB + 1]).then_inc(net_sb, 1)
            act.wait_ge(net_sb, 6)
            act.activation(gpos[:], graw[:], ACT.Relu).then_inc(soft_steps, 1)
            act.activation(gneg[:], graw[:], ACT.Relu, scale=-1.0).then_inc(soft_steps, 1)
            act.wait_ge(gabs_ready, 1)
            act.activation(gexp[:], gabs[:], ACT.Exp, scale=-1.0).then_inc(soft_steps, 1)
            act.wait_ge(soft_steps, 3)
            act.activation(glog[:], gexp[:], ACT.Ln, bias=one[:, 0:1]).then_inc(soft_steps, 1)
            act.activation(table[:], one[:], ACT.Sqrt)

            def relu_step():
                for b in range(BH, B, 2):
                    act.wait_ge(xp_ready, b + 2)
                    act.activation(xs[:, b:b + 2, :], xp[:, b:b + 2, :], ACT.Relu).then_inc(xs_act_ready, 1)

            def sd_features(n):
                act.wait_ge(var1_ready, BH * (n + 1))
                act.activation(sd1[:, n * BH:(n + 1) * BH], mv1[:, n * BH:(n + 1) * BH, 1], ACT.Sqrt,
                               bias=eps_ln[:, 0:1]).then_inc(sd1_ready, 1)

            def normalise(n):
                act.wait_ge(rs1_ready, 2 * (n + 1))
                for b in range(n * BH + XN_DVE[n], (n + 1) * BH):
                    act.activation(xn[:, b, :], xs[:, b, :], ACT.Identity, bias=mrs1[:, b:b + 1],
                                   scale=rs1[:, b:b + 1]).then_inc(xn_act_ready, 1)

            def sd_tokens(n):
                act.wait_ge(var2_ready, n + 1)
                act.activation(sd2[:, n * BH:(n + 1) * BH], vh[:, n * BH:(n + 1) * BH], ACT.Sqrt,
                               bias=eps_t[:, 0:1]).then_inc(sd2_ready, 1)

            def conditioned(n):
                act.wait_ge(shift_ready, 2 * (n + 1))
                for b in range(H_DVE[n], BH):
                    bb = n * BH + b
                    act.activation(h[:, bb * P:(bb + 1) * P], xnT(n, b), ACT.Identity,
                                   bias=shift[:, bb:bb + 1], scale=scale[:, bb:bb + 1]).then_inc(h_act_ready, 1)

            def transposed_step(n):
                act.wait_ge(xsT_ready, n + 1)
                act.activation(acc[:, n * HT:(n + 1) * HT], xsT[n], ACT.Copy).then_inc(acc_ready, 1)

            def hidden_high(c, n):
                tok = slice(n * HT, (n + 1) * HT)
                act.wait_ge((z_early_ready, z_ready)[n], c + 1)
                ins = act.activation(hid_hi[:, c, tok], zt[c][:, tok], ACT.Relu, bias=b1s[:, 0, c:c + 1])
                if n == 1:
                    ins.then_inc(hi_ready, 1)

            def hidden_whole(c, n):
                tok = slice(n * HT, (n + 1) * HT)
                act.activation(hid[:, c, tok], zt[c][:, tok], ACT.Relu,
                               bias=b1s[:, 0, c:c + 1]).then_inc((hid_early_ready, hid_ready)[n], 1)

            sd_features(0)
            normalise(0)
            relu_step()
            sd_tokens(0)
            for n in range(HALVES):
                transposed_step(n)
            sd_features(1)
            normalise(1)
            conditioned(0)
            act.wait_ge(h_ready, 2)
            act.wait_ge(h_act_ready, 2)
            act.activation(h_hi[:, 0:HT], h[:, 0:HT], ACT.Copy).then_inc(h_hi_ready[0], 1)
            sd_tokens(1)
            conditioned(1)
            act.wait_ge(b1_ready, 1)
            hidden_high(0, 0)
            hidden_whole(0, 0)
            hidden_high(1, 0)
            hidden_whole(1, 0)

            def hidden(e, c, slot, start):
                g = C * e + c
                act.wait_ge(z_ready, g + 1)
                if not start:
                    if c < C - 1:
                        act.wait_ge(l2_done, (C - 1) * (e - 1) + c + 1)
                    else:
                        act.wait_ge(y_half, HALVES * e)
                bias = b1s[:, slot, c:c + 1]
                if c == 0:
                    act.wait_ge(b1_ready, e + 1)
                act.activation(hid_hi[:, c, :], zt[c % 2][:], ACT.Relu, bias=bias).then_inc(hi_ready, 1)
                if not start:
                    act.wait_ge(lo_ready, g - C + 1)
                act.activation(hid[:, c, :], zt[c % 2][:], ACT.Relu, bias=bias).then_inc(hid_ready, 1)

            def last_hidden():
                c = C - 1
                act.wait_ge(y_half, HALVES * (E - 1))
                act.wait_ge(lo_ready, C * (E - 1))
                for n in range(HALVES):
                    tok = slice(n * HT, (n + 1) * HT)
                    z_ps, bias = zt[c % 2][:, tok], b1s[:, (E - 1) % SLOTS, c:c + 1]
                    act.wait_ge(z_last_ready, n + 1)
                    act.activation(hid_hi[:, c, tok], z_ps, ACT.Relu, bias=bias).then_inc(hi_ready, 1)
                    act.activation(hid[:, c, tok], z_ps, ACT.Relu, bias=bias).then_inc(hid_ready, 1)

            def pair(i, first=False, final=False):
                for k in range(2):
                    e = 2 * i + k
                    for c in range(C):
                        if first and k == 0 and c < 2:
                            if c == 1:
                                act.wait_ge(hid_ready, 2)
                            hidden_high(c, 1)
                            if c == 0:
                                hidden_whole(c, 1)
                        elif final and k == 1 and c == C - 1:
                            last_hidden()
                        else:
                            hidden(e, c, k, first and k == 0)
                        if first and k == 0 and c == 0:
                            act.wait_ge(ld_ready, 1)
                            act.activation(pe_[:], ld[:], ACT.Exp).then_inc(exp_ready, 1)
                        if first and k == 0 and c == C - 1:
                            act.wait_ge(gateT_ps, 1)
                            act.activation(gateT[:], aux[0:E, :], ACT.Copy).then_inc(gateT_ready, 1)
            pair(0, first=True)
            with act.Fori(1, E // 2 - 1) as i:
                pair(i)
            pair(E // 2 - 1, final=True)

        @block.tensor
        def _(pe):
            def net_layer(n, weights, acts, rows):
                pe.matmul(small[0:rows, 0:B], weights, acts, start=True, stop=True).then_inc(net_ps, 1)

            def step_cross(n):
                if n == 0:
                    pe.wait_ge(first_in, 16)
                pe.wait_ge(s_ready, n + 1)
                for b in range(BH):
                    if n == 0 and b == 2:
                        pe.wait_ge(onehot_ready, 1)
                        pe.wait_ge(p64_in, 16)
                        net_layer(0, pw[0:NS, EMB_AT:EMB_AT + SE], onehot[:], SE)
                    last = pe.matmul(rT[n][:, b * P:(b + 1) * P], s_b2[:, n * BH + b, :], diff,
                                     start=True, stop=True)
                last.then_inc(rT_ready, 1)

            def step_rows(m):
                pe.wait_ge(rows_hi_ready, m + 1)
                pe.matmul(df[0], diffs[:, m, :], rows_hi[:, m].rearrange("p b j -> p (b j)"),
                          start=(m == 0), stop=False, skip_group_check=True)
                pe.wait_ge(rows_lo_ready, m + 1)
                pe.matmul(df[0], diffs[:, m, :], rows_lo[:, m].rearrange("p b j -> p (b j)"),
                          start=False, stop=False, skip_group_check=True)

            def step_rows_float32():
                pe.wait_ge(a0_ready, 2)
                pe.matmul(df[1], diff, u_a0[:, BH:B, :].rearrange("p b j -> p (b j)"),
                          start=True, stop=False, skip_group_check=True)
                pe.wait_ge(b_ready, 3)
                pe.matmul(df[1], mats[:, HALF_DIFF2, :], u_b0[:, BH:B, :].rearrange("p b j -> p (b j)"),
                          start=False, stop=False, skip_group_check=True)

            def step_columns_w(n):
                pe.wait_ge(w_op_ready, n + 1)
                for b in range(BH):
                    pe.matmul(df[n][:, b * P:(b + 1) * P], wT[:, n * BH + b, :], diff,
                              start=False, stop=False, skip_group_check=True)

            def step_columns_b(n):
                pe.wait_ge(b_ready, 2 * n + 2)
                for b in range(BH):
                    last = pe.matmul(df[n][:, b * P:(b + 1) * P], u_b1[:, n * BH + b, :], mats[:, HALF_DIFF2, :],
                                     start=False, stop=(b == BH - 1), skip_group_check=True)
                last.then_inc(df_ready, 1)

            def keep_warm(count):
                for _ in range(count):
                    pe.matmul(warm_ps, warm[:, 0:P], warm[:], start=True, stop=True)

            pe.wait_ge(warm_ready, 1)
            keep_warm(WARM_START)
            step_cross(0)
            pe.wait_ge(net_sb, 1)
            net_layer(1, pw[:, HW1_AT:HW1_AT + SH], se[:], SH)
            pe.wait_ge(diffs_ready, 1)
            step_rows(0)
            pe.wait_ge(p128_in, 16)
            pe.wait_ge(net_sb, 2)
            net_layer(2, pv[:, HW2_AT:HW2_AT + SH], hyp1[:], SH)
            pe.wait_ge(diffs_ready, 2)
            step_rows(1)
            pe.wait_ge(net_sb, 3)
            net_layer(3, pv[:, SW1_AT:SW1_AT + SE], hyp2[:], SE)
            step_columns_w(0)
            pe.wait_ge(net_sb, 4)
            pe.matmul(small[:, 0:B], pw[:, SW2_AT:SW2_AT + P], sty1[:], start=True, stop=True)
            pe.matmul(small[:, B:2 * B], pw[:, SW2_AT + P:SW2_AT + 2 * P], sty1[:], start=True,
                      stop=True).then_inc(net_ps, 1)
            step_columns_b(0)
            step_cross(1)
            step_rows_float32()
            step_columns_w(1)
            step_columns_b(1)

            def step_transposed(n):
                if n == 0:
                    pe.wait_ge(xs_ready, 1)
                else:
                    pe.wait_ge(xs_act_ready, 2)
                for b in range(BH):
                    last = pe.transpose(xsT[n][:, b * P:(b + 1) * P], xs[:, n * BH + b, :], ident)
                last.then_inc(xsT_ready, 1)

            def norm_transposed(n):
                if n == 0:
                    pe.wait_ge(net_sb, 6)
                for b in range(BH):
                    by_dve = XN_DVE[n]
                    if b < by_dve:
                        pe.wait_ge(xn_ready, sum(XN_DVE[:n]) + b + 1)
                    else:
                        pe.wait_ge(xn_act_ready, BH * n - sum(XN_DVE[:n]) + b - by_dve + 1)
                    last = pe.transpose(xnT(n, b), xn[:, n * BH + b, :], ident)
                    if b % 2 == 1:
                        last.then_inc(xnT_ready, 1)

            def logits(n):
                pe.wait_ge(h_act_ready, BH * (n + 1) - sum(H_DVE[:n + 1]))
                if H_DVE[n]:
                    pe.wait_ge(h_ready, sum(H_DVE[:n + 1]))
                for b in range(n * BH, (n + 1) * BH):
                    last = pe.matmul(lg_ps[:, b * E:(b + 1) * E], h[:, b * P:(b + 1) * P], pv[:, RW_AT:RW_AT + E],
                                     start=True, stop=True)
                last.then_inc(logits_ready, 1)

            norm_transposed(0)
            for n in range(HALVES):
                step_transposed(n)
            keep_warm(WARM_NORM)
            norm_transposed(1)

            def layer1_half(c, slot, n):
                tok = slice(n * HT, (n + 1) * HT)
                w_hi, w_lo = ws[:, slot, 0, 0, c, :], ws[:, slot, 1, 0, c, :]
                pe.matmul(zt[c % 2][:, tok], w_hi, h_hi[:, tok], start=True, stop=False)
                pe.matmul(zt[c % 2][:, tok], w_lo, h_hi[:, tok], start=False, stop=False)
                return pe.matmul(zt[c % 2][:, tok], w_hi, h_lo[:, tok], start=False, stop=True)

            def layer1(e, c, slot, between=None):
                if c == 0:
                    pe.wait_ge(w_ready, e + 1)
                layer1_half(c, slot, 0)
                if between is not None:
                    between()
                layer1_half(c, slot, 1).then_inc(z_ready, 1)

            def share(out_ps, tok, c, slot, wait_for_low=None):
                w_hi, w_lo = ws[:, slot, 0, 1, c, :], ws[:, slot, 1, 1, c, :]
                pe.matmul(out_ps, w_hi, hid_hi[:, c, tok], start=(c == 0), stop=False)
                pe.matmul(out_ps, w_lo, hid_hi[:, c, tok], start=False, stop=False)
                if wait_for_low is not None:
                    pe.wait_ge(*wait_for_low)
                return pe.matmul(out_ps, w_hi, hid_lo[:, c, tok], start=False, stop=(c == C - 1))

            def layer2(e, c, slot, first, parts):
                pe.wait_ge(hi_ready, C * e + c + 1)
                for p, (out_ps, tok) in enumerate(parts):
                    if c == 0 and not first:
                        pe.wait_ge(yg_half, HALVES * (e - 1) + min(p, 1) + 1)
                    last = share(out_ps, tok, c, slot, (lo_ready, C * e + c + 1) if p == 0 else None)
                    if c == C - 1:
                        last.then_inc(y_half, 1)
                if c < C - 1:
                    last.then_inc(l2_done, 1)

            def last_layer2():
                slot = (E - 1) % SLOTS
                for p, (out_ps, tok) in enumerate(y_last):
                    n = min(p, 1)
                    pe.wait_ge(hi_ready, C * E - 1)
                    share(out_ps, tok, C - 2, slot, (lo_ready, C * E - 1))
                    pe.wait_ge(hi_ready, C * E + n)
                    share(out_ps, tok, C - 1, slot, (lo_ready, C * E + n)).then_inc(y_last_ready, 1)

            def gates_transposed():
                pe.wait_ge(gates_ready, 1)
                for b in range(B):
                    last = pe.transpose(aux[0:E, b * P:(b + 1) * P], gate[:, b, :], ident)
                last.then_inc(gateT_ps, 1)

            def pair(i, first=False, final=False):
                for k in range(2 * C - 2 if final else 2 * C):
                    e, c = 2 * i + k // C, k % C
                    start = first and k < C
                    if start and c == 0:
                        pe.wait_ge(hi_ready, 1)
                        share(*y_halves[1], 0, 0, (lo_ready, 1)).then_inc(l2_done, 1)
                    else:
                        layer2(e, c, k // C, start, y_last if final and k >= C else y_halves)
                    if k + LAG < 2 * C or not final:
                        ahead = k + LAG
                        e1, c1 = 2 * i + ahead // C, ahead % C
                        pe.wait_ge(hid_ready, C * e1 + c1 - 1)
                        if start and c == 0:
                            pe.wait_ge(hi_ready, 2)
                        if final and ahead == 2 * C - 1:
                            for n in range(HALVES):
                                layer1_half(c1, 1, n).then_inc(z_last_ready, 1)
                        else:
                            layer1(e1, c1, (ahead // C) % SLOTS,
                                   gates_transposed if start and c == GATES_AT else None)

            keep_warm(WARM_HALF)
            pe.wait_ge(w_ready, 1)
            pe.wait_ge(acc_ready, HALVES)
            w_hi, w_lo = ws[:, 0, 0, 0], ws[:, 0, 1, 0]
            for n in range(HALVES):
                tok = slice(n * HT, (n + 1) * HT)
                pe.wait_ge(h_hi_ready[n], n + 1)
                for c in range(2):
                    pe.matmul(zt[c][:, tok], w_hi[:, c, :], h_hi[:, tok], start=True, stop=False)
                    pe.matmul(zt[c][:, tok], w_lo[:, c, :], h_hi[:, tok], start=False, stop=False)
                pe.wait_ge(h_lo_ready[n], 1)
                for c in range(2):
                    pe.matmul(zt[c][:, tok], w_hi[:, c, :], h_lo[:, tok], start=False,
                              stop=True).then_inc((z_early_ready, z_ready)[n], 1)
                if n == 0:
                    logits(0)
            logits(1)
            pe.wait_ge(hid_early_ready, 1)
            pe.wait_ge(lo_early_ready, 1)
            share(*y_halves[0], 0, 0)
            pe.wait_ge(hid_ready, 1)
            layer1(0, 2, 0)
            pair(0, first=True)
            with pe.Fori(1, E // 2 - 1) as i:
                pair(i)
            pair(E // 2 - 1, final=True)
            last_layer2()

        @block.vector
        def _(v):
            count = [0]

            def mark(ins):
                count[0] += 1
                ins.then_inc(dve, 1)
                return count[0]

            def then(ins):
                v.wait_ge(dve, mark(ins))

            v.memset(warm[:], 0.0).then_inc(warm_ready, 1)
            v.memset(eps_ln[:], 1e-5).then_inc(const_ready, 1)
            v.memset(eps_t[:], 1e-8).then_inc(const_ready, 1)
            v.memset(one[:], 1.0).then_inc(const_ready, 1)

            def row_low_parts(m):
                v.wait_ge(rows_hi_ready, m + 1)
                v.tensor_tensor(rows_lo[:, m], (u_a0, u_b0)[m][:, 0:BH, :], rows_hi[:, m].bitcast(F32),
                                ALU.subtract).then_inc(rows_lo_ready, 1)

            def operands(n):
                hb = slice(n * BH, (n + 1) * BH)
                v.wait_ge(f_in[n], 16)
                if n == 0:
                    v.wait_ge(first_in, 16)
                v.tensor_tensor(s_b2[:, hb, :], f[:, hb, :], over_batches(b2_grid), ALU.mult).then_inc(s_ready, 1)
                if n == 0:
                    v.wait_ge(gn_in, 16)
                    then(v.tensor_scalar(neg_a0[:], gn[:, 0, :], -1.0, None, ALU.mult))
                v.tensor_tensor(u_a0[:, hb, :], f[:, hb, :], over_batches(neg_a0[:]), ALU.mult).then_inc(a0_ready, 1)
                if n == 0:
                    v.tensor_copy(diffs[:, 0, :], diff).then_inc(diffs_ready, 1)
                v.wait_ge(gt_in, 16)
                v.wait_ge(ft_in[n], 16)
                v.tensor_tensor(u_a1[:, hb, :], ft[:, hb, :], over_batches(gt[:, 1, :]), ALU.mult).then_inc(a1_ready, 1)

            def cross_operand(n):
                hb = slice(n * BH, (n + 1) * BH)
                v.wait_ge(a1_ready, n + 1)
                v.wait_ge(rT_ready, n + 1)
                v.tensor_tensor(wT[:, hb, :], rT[n].rearrange("p (b j) -> p b j", b=BH), u_a1[:, hb, :],
                                ALU.subtract).then_inc(w_op_ready, 1)

            def advance(n):
                v.wait_ge(dt_in, 16)
                v.wait_ge(df_ready, n + 1)
                for b in range(BH):
                    bb = n * BH + b
                    v.scalar_tensor_tensor(xp[:, bb, :], df[n][:, b * P:(b + 1) * P], dtb[:, bb:bb + 1], f[:, bb, :],
                                           ALU.mult, ALU.add).then_inc(xp_ready, 1)

            def feature_stats(batches):
                for bb in batches:
                    if bb >= BH:
                        v.wait_ge(xs_act_ready, (bb - BH) // 2 + 1)
                    last = mark(v.bn_stats(st1[:, bb, :], xs[:, bb, :]))
                return last

            def feature_means(n, stats):
                v.wait_ge(dve, stats)
                for bb in range(n * BH, (n + 1) * BH):
                    v.bn_aggr(mv1[:, bb, :], st1[:, bb, :]).then_inc(var1_ready, 1)

            def one_over_sd(n):
                hb = slice(n * BH, (n + 1) * BH)
                v.wait_ge(sd1_ready, n + 1)
                v.reciprocal(rs1[:, hb], sd1[:, hb]).then_inc(rs1_ready, 1)

            def normalise(n):
                hb = slice(n * BH, (n + 1) * BH)
                v.wait_ge(var1_ready, BH * (n + 1))
                v.wait_ge(rs1_ready, 2 * n + 1)
                for k in range(XN_DVE[n]):
                    bb = n * BH + k
                    v.tensor_scalar(xn[:, bb, :], xs[:, bb, :], mv1[:, bb, 0:1], rs1[:, bb:bb + 1],
                                    ALU.subtract, ALU.mult).then_inc(xn_ready, 1)
                    if k == 0:
                        v.scalar_tensor_tensor(mrs1[:, hb], mv1[:, hb, 0], -1.0, rs1[:, hb], ALU.mult,
                                               ALU.mult).then_inc(rs1_ready, 1)

            def token_stats(n):
                for b in range(BH):
                    v.wait_ge(xnT_ready, 2 * n + b // 2 + 1)
                    last = mark(v.bn_stats(st2[:, n * BH + b, :], xnT(n, b)))
                v.wait_ge(dve, last)
                for bb in range(n * BH, (n + 1) * BH):
                    last = mark(v.bn_aggr(mv2[:, bb, :], st2[:, bb, :]))
                v.wait_ge(dve, last)
                hb = slice(n * BH, (n + 1) * BH)
                v.tensor_scalar(vh[:, hb], mv2[:, hb, 1], gsq[:, 0:1], None, ALU.mult).then_inc(var2_ready, 1)
                return mark(v.tensor_scalar(mh[:, hb], mv2[:, hb, 0], g, b0, ALU.mult, ALU.add))

            def less_mean(n, mean):
                hb = slice(n * BH, (n + 1) * BH)
                v.wait_ge(dve, mean)
                return mark(v.tensor_scalar(dmean[:, hb], mh[:, hb], -1.0, b0, ALU.mult, ALU.add))

            def less_mean_gamma(n, less):
                hb = slice(n * BH, (n + 1) * BH)
                v.wait_ge(dve, less)
                if n == 0:
                    v.wait_ge(gamma_ready, 2)
                    v.wait_ge(net_sb, 6)
                return mark(v.tensor_tensor(tg[:, hb], dmean[:, hb], gamma[:, hb], ALU.mult))

            def one_over_sd_tokens(n):
                hb = slice(n * BH, (n + 1) * BH)
                v.wait_ge(sd2_ready, n + 1)
                return mark(v.reciprocal(rs2[:, hb], sd2[:, hb]))

            def scale_and_shift(n, product, inverse):
                hb = slice(n * BH, (n + 1) * BH)
                v.wait_ge(dve, inverse)
                v.tensor_tensor(scale[:, hb], rs2[:, hb], gamma_g[:, hb], ALU.mult).then_inc(shift_ready, 1)
                v.wait_ge(dve, product)
                return mark(v.tensor_tensor(shift0[:, hb], tg[:, hb], rs2[:, hb], ALU.mult))

            def plus_beta(n, shifted):
                hb = slice(n * BH, (n + 1) * BH)
                v.wait_ge(dve, shifted)
                v.tensor_tensor(shift[:, hb], shift0[:, hb], beta[:, hb], ALU.add).then_inc(shift_ready, 1)

            def conditioned(n):
                v.wait_ge(shift_ready, 2 * (n + 1))
                for b in range(H_DVE[n]):
                    bb = n * BH + b
                    v.tensor_scalar(h[:, bb * P:(bb + 1) * P], xnT(n, b), scale[:, bb:bb + 1], shift[:, bb:bb + 1],
                                    ALU.mult, ALU.add).then_inc(h_ready, 1)

            def input_parts():
                tok = slice(HT, T)
                own = slice(HT, HT + H_DVE[1] * P)
                v.wait_ge(h_ready, sum(H_DVE))
                v.tensor_copy(h_hi[:, own], h[:, own]).then_inc(h_hi_ready[1], 1)
                v.wait_ge(h_act_ready, B - sum(H_DVE))
                v.tensor_copy(h_hi[:, own.stop:T], h[:, own.stop:T]).then_inc(h_hi_ready[1], 1)
                v.wait_ge(h_hi_ready[1], 2)
                v.tensor_tensor(h_lo[:, tok], h[:, tok], h_hi[:, tok].bitcast(F32),
                                ALU.subtract).then_inc(h_lo_ready[1], 1)

            def router_start():
                v.wait_ge(logits_ready, HALVES)
                lg = lg_ps[:, 0:B * E].rearrange("p (b e) -> p b e", e=E)
                then(v.tensor_reduce(lmax[:], lg, AX.X, ALU.max))
                v.tensor_tensor(ld[:], lg, per_expert(lmax), ALU.subtract).then_inc(ld_ready, 1)

            def router():
                v.wait_ge(exp_ready, 1)
                then(v.tensor_reduce(z[:], pe_[:], AX.X, ALU.add))
                then(v.reciprocal(rz[:], z[:]))
                then(v.tensor_tensor(pr[:], pe_[:], per_expert(rz), ALU.mult))
                for b in range(B):
                    last = mark(v.max(top8[:, b, :], pr[:, b, :]))
                return last

            def top_two(last):
                v.wait_ge(dve, last)
                then(v.tensor_tensor(ps[:], top8[:, :, 0], top8[:, :, 1], ALU.add))
                mark(v.reciprocal(rps[:], ps[:]))
                then(v.memset(top8[:, :, TOPK:E], -1.0))
                for b in range(B):
                    last = mark(v.match_replace(rest[:, b, :], top8[:, b, :], pr[:, b, :], 0.0))
                v.wait_ge(dve, last)
                then(v.tensor_tensor(pk[:], pr[:], rest[:], ALU.subtract))
                v.tensor_tensor(gate[:], pk[:], per_expert(rps), ALU.mult).then_inc(gates_ready, 1)

            operands(0)
            row_low_parts(0)
            v.wait_ge(mats_in, 16)
            v.tensor_copy(diffs[:, 1, :], mats[:, HALF_DIFF2, :]).then_inc(diffs_ready, 1)
            row_low_parts(1)
            cross_operand(0)
            operands(1)
            v.wait_ge(p128_in, 16)
            v.tensor_copy(b1s[:, 0, :], pv[:, BIAS_AT:BIAS_AT + NB]).then_inc(b1_ready, 1)
            g, b0 = pv[:, LN_G:LN_G + 1], pv[:, LN_B:LN_B + 1]
            squared = mark(v.tensor_scalar(gsq[:], g, g, None, ALU.mult))
            advance(0)
            cross_operand(1)
            v.wait_ge(xp_ready, BH)
            v.tensor_scalar(xs[:, 0:BH, :], xp[:, 0:BH, :], 0.0, None, ALU.max).then_inc(xs_ready, 1)
            v.wait_ge(xs_ready, 1)
            feature_means(0, feature_stats(range(BH)))
            one_over_sd(0)
            normalise(0)
            advance(1)
            v.wait_ge(dve, squared)
            mean = token_stats(0)
            feature_stats(range(BH, BH + 1))
            less = less_mean(0, mean)
            feature_stats(range(BH + 1, BH + 2))
            product = less_mean_gamma(0, less)
            stats = feature_stats(range(BH + 2, B))
            inverse = one_over_sd_tokens(0)
            feature_means(1, stats)
            shifted = scale_and_shift(0, product, inverse)
            one_over_sd(1)
            plus_beta(0, shifted)
            normalise(1)
            conditioned(0)
            less = less_mean(1, token_stats(1))
            inverse = one_over_sd_tokens(1)
            product = less_mean_gamma(1, less)
            plus_beta(1, scale_and_shift(1, product, inverse))
            conditioned(1)
            input_parts()
            for c in range(2):
                v.wait_ge(hid_early_ready, c + 1)
                v.tensor_tensor(hid_lo[:, c, 0:HT], hid[:, c, 0:HT], hid_hi[:, c, 0:HT].bitcast(F32),
                                ALU.subtract).then_inc(lo_early_ready, 1)
            router_start()
            v.wait_ge(z_ready, 2)
            v.wait_ge(hid_ready, 1)
            v.tensor_scalar(hid[:, 1, HT:T], zt[1][:, HT:T], b1s[:, 0, 1:2], 0.0, ALU.add,
                            ALU.max).then_inc(hid_ready, 1)

            def low_part(e, c, start):
                g = C * e + c
                v.wait_ge(hi_ready, g + 1)
                v.wait_ge(hid_ready, g + 1)
                if start and c < 2:
                    v.tensor_tensor(hid_lo[:, c, HT:T], hid[:, c, HT:T], hid_hi[:, c, HT:T].bitcast(F32),
                                    ALU.subtract).then_inc(lo_ready, 1)
                    return
                if not start:
                    if c < C - 1:
                        v.wait_ge(l2_done, (C - 1) * (e - 1) + c + 1)
                    else:
                        v.wait_ge(y_half, HALVES * e)
                v.tensor_tensor(hid_lo[:, c, :], hid[:, c, :], hid_hi[:, c, :].bitcast(F32),
                                ALU.subtract).then_inc(lo_ready, 1)

            def split_weights(e, slot):
                v.wait_ge(y_half, HALVES * (e - 1))
                src = we[:, bass.ds(e, 1)].rearrange("p o l c m -> p (o l c m)")
                hi = ws[:, slot, 0].rearrange("p l c m -> p (l c m)")
                lo = ws[:, slot, 1].rearrange("p l c m -> p (l c m)")
                v.tensor_copy(hi, src).then_inc(w_hi_ready, 1)
                v.wait_ge(w_hi_ready, e - 1)
                v.tensor_tensor(lo, src, hi.bitcast(F32), ALU.subtract).then_inc(w_ready, 1)

            def biases(e, slot, first):
                if not first:
                    v.wait_ge(hid_ready, C * (e - 1))
                    v.wait_ge(yg_half, HALVES * (e - 1))
                v.tensor_copy(b1s[:, slot, :], pv[:, bass.ds(BIAS_AT + NB * e, NB)]).then_inc(b1_ready, 1)

            def add_up(e, first):
                for n in range(HALVES):
                    tok = slice(n * HT, (n + 1) * HT)
                    v.wait_ge(yg_half, HALVES * e + n + 1)
                    if first:
                        v.wait_ge(acc_ready, HALVES)
                    else:
                        v.wait_ge(acc_half, HALVES * e)
                    v.tensor_tensor(acc[:, tok], acc[:, tok], yg[:, tok], ALU.add).then_inc(acc_half, 1)

            def gated(e, slot, used, first):
                v.wait_ge(gate_ready[slot], 16 * used)
                if not first:
                    v.wait_ge(acc_half, HALVES * e)
                for n in range(HALVES):
                    tok = slice(n * HT, (n + 1) * HT)
                    v.wait_ge(y_half, HALVES * e + n + 1)
                    v.scalar_tensor_tensor(yg[:, tok], yt[:, tok], b1s[:, slot, C:NB], gate_all[:, slot, tok], ALU.add,
                                           ALU.mult).then_inc(yg_half, 1)

            def pair(i, first=False, final=False):
                for k in range(2):
                    e = 2 * i + k
                    start = first and k == 0
                    low_part(e, 0, start)
                    if not start:
                        gated(e - 1, (k + 1) % SLOTS, i + k, first)
                    if start:
                        sorted_ready = router()
                    low_part(e, 1, start)
                    if start:
                        top_two(sorted_ready)
                    if not (final and k == 1):
                        biases(e + 1, (k + 1) % SLOTS, start)
                        if not start:
                            split_weights(e + 1, (k + 1) % SLOTS)
                    if final and k == 1:
                        add_up(e - 1, first)
                    low_part(e, 2, start)
                    if not (start or final and k == 1):
                        add_up(e - 1, first)
                    if not (final and k == 1):
                        low_part(e, 3, start)

            v.wait_ge(w_in[2], 16 * (E - 2))
            pair(0, first=True)
            with v.Fori(1, E // 2 - 1) as i:
                pair(i)
            pair(E // 2 - 1, final=True)
            v.wait_ge(y_half, HALVES * (E - 1))
            for n in range(HALVES):
                tok = slice(n * HT, (n + 1) * HT)
                v.wait_ge(hi_ready, C * E + n)
                v.wait_ge(hid_ready, C * E + n)
                v.tensor_tensor(hid_lo[:, C - 1, tok], hid[:, C - 1, tok], hid_hi[:, C - 1, tok].bitcast(F32),
                                ALU.subtract).then_inc(lo_ready, 1)
            slot = (E - 1) % SLOTS
            v.wait_ge(gate_ready[slot], 16 * E // SLOTS)
            v.wait_ge(acc_half, HALVES * (E - 1))

            def gated_part(p):
                out_ps, tok = y_last[p]
                v.wait_ge(y_last_ready, p + 1)
                v.scalar_tensor_tensor(yg[:, tok], out_ps, b1s[:, slot, C:NB], gate_all[:, slot, tok], ALU.add,
                                       ALU.mult).then_inc(yg_last_ready, 1)

            def added_part(p):
                tok = y_last[p][1]
                v.wait_ge(yg_last_ready, p + 1)
                v.tensor_tensor(acc[:, tok], acc[:, tok], yg[:, tok], ALU.add).then_inc(out_ready[p], 1)

            gated_part(0)
            gated_part(1)
            gated_part(2)
            added_part(1)
            added_part(2)


def kernel(**inputs):
    import concourse.bacc as bacc
    from concourse.bass_utils import run_bass_kernel_spmd

    given = {name.removeprefix("L0_cond_").removeprefix("L1_cond_"): np.ascontiguousarray(a)
             for name, a in inputs.items()}
    x, a_grid, b_grid = given["x"], given["A_grid"], given["B_grid"]
    diff, mats = constants()
    expert_biases = np.concatenate([given["exp_b1"].reshape(E, C, P), given["exp_b2"][:, None, :]], axis=1)
    expert_biases = expert_biases.transpose(2, 0, 1).reshape(P, E * NB)
    p128 = np.concatenate(
        [np.stack([given[n] for n in ("ln_g", "ln_b", "hyp_b1", "hyp_b2")], axis=1), given["sty_b2"].reshape(2, P).T,
         given["router_w"], given["hyp_w2"], given["sty_w1"], expert_biases], axis=1)
    emb = np.zeros((SE, SE), np.float32)
    emb[0:NS] = given["subj_emb"]
    p64 = np.concatenate([given["sty_b1"][:, None], given["hyp_w1"], given["sty_w2"], emb], axis=1)
    exp_w = np.stack([given["exp_w1"].reshape(E, P, C, P), given["exp_w2"].reshape(E, C, P, P).transpose(0, 2, 1, 3)],
                     axis=2)
    tensors = {
        "grid_and_difference": np.stack([b_grid[2], diff], axis=1), "matrices": mats,
        "x": x.transpose(1, 0, 2), "x_exchanged": x.transpose(2, 0, 1),
        "grids": np.stack([a_grid[0], b_grid[0]], axis=1),
        "grids_exchanged": np.stack([b_grid[1].T, a_grid[1].T], axis=1),
        "dt": given["condB_dt"], "ids": given["itok_B_6_14"],
        "parameters_128": p128, "parameters_64": p64, "exp_w": exp_w,
    }
    nc = bacc.Bacc("TRN2", target_bir_lowering=False, num_devices=1)
    arrays, args = {}, []
    for name, a in tensors.items():
        arrays[f"in_{name}_dram"] = a = np.ascontiguousarray(a)
        args.append(nc.dram_tensor(f"in_{name}_dram", a.shape, mybir.dt.from_np(a.dtype), kind="ExternalInput").ap())
    out = nc.dram_tensor("out_0_dram", (P, T), F32, kind="ExternalOutput").ap()
    build(nc, *args, out)
    got = run_bass_kernel_spmd(nc, [arrays], core_ids=[0]).results[0]["out_0_dram"]
    return np.ascontiguousarray(got.reshape(P, B, P).transpose(1, 2, 0))
```
